# Optimizing a Trainium2 kernel written in Bass

```python
import numpy as np
import jax
import jax.numpy as jnp

def _softmax(x, axis=-1):
    return jax.nn.softmax(x, axis=axis)

def _gelu(x):
    return jax.nn.gelu(x, approximate=True)

def _silu(x):
    return jax.nn.silu(x)

def _sigmoid(x):
    return jax.nn.sigmoid(x)

def _layernorm(x, axis=-1, eps=1e-05):
    m = jnp.mean(x, axis=axis, keepdims=True)
    v = jnp.var(x, axis=axis, keepdims=True)
    return (x - m) / jnp.sqrt(v + eps)

def _scatter_add(tgt, idx, src, axis=0):
    return tgt.at[idx].add(src)

def _segment_sum(src, seg, n):
    return jax.ops.segment_sum(src, seg, n)
kernel_name = 'mk_vit_tower_d1_tok_img256_r4_a072bf'

def setup_inputs(seed: int=0):
    np.random.seed(seed)
    _w = jnp.asarray

    def _rec_inputs():
        import jax
        import jax.numpy as jnp
        _rk = jax.random.key(seed)
        x = -0.000596345 + 1.00056 * jax.random.normal(jax.random.fold_in(_rk, 1), (128, 64, 64, 3), jnp.float32)
        return x
    x = _rec_inputs()

    def _L0_tok_setup():
        import jax, jax.numpy as jnp
        import numpy as np
        M1, M2, WIDTH, LAYERS = (16, 16, 64, 4)
        B, H, W = (16, 64, 64)
        EPS = 1e-05

        def _spectral_conv(h, w1, w2):
            xf = jnp.fft.rfft2(h)
            top = jnp.einsum('bixy,ioxy->boxy', xf[:, :, :M1, :M2], w1)
            bot = jnp.einsum('bixy,ioxy->boxy', xf[:, :, -M1:, :M2], w2)
            of = jnp.zeros(xf.shape, dtype=xf.dtype)
            of = of.at[:, :, :M1, :M2].set(top)
            of = of.at[:, :, -M1:, :M2].set(bot)
            return jnp.fft.irfft2(of, s=(h.shape[-2], h.shape[-1]))
        key = jax.random.key(seed)
        ks = jax.random.split(key, 16)
        scale = 1.0 / (WIDTH * WIDTH)
        inp = {'x': jax.random.normal(ks[0], (B, H, W, 3), dtype=jnp.float32), 'fc0_w': jax.random.normal(ks[1], (3, WIDTH), dtype=jnp.float32) * 0.3, 'fc0_b': jnp.zeros((WIDTH,), jnp.float32), 'w1r': jax.random.normal(ks[2], (LAYERS, WIDTH, WIDTH, M1, M2), dtype=jnp.float32) * scale, 'w1i': jax.random.normal(ks[3], (LAYERS, WIDTH, WIDTH, M1, M2), dtype=jnp.float32) * scale, 'w2r': jax.random.normal(ks[4], (LAYERS, WIDTH, WIDTH, M1, M2), dtype=jnp.float32) * scale, 'w2i': jax.random.normal(ks[5], (LAYERS, WIDTH, WIDTH, M1, M2), dtype=jnp.float32) * scale, 'pw_w': jax.random.normal(ks[6], (LAYERS, WIDTH, WIDTH), dtype=jnp.float32) * (1.0 / np.sqrt(WIDTH)), 'pw_b': jnp.zeros((LAYERS, WIDTH), jnp.float32), 'gamma': jnp.ones((LAYERS, WIDTH), jnp.float32), 'beta': jnp.zeros((LAYERS, WIDTH), jnp.float32), 'fc1_w': jax.random.normal(ks[7], (WIDTH, 128), dtype=jnp.float32) * (1.0 / np.sqrt(WIDTH)), 'fc1_b': jnp.zeros((128,), jnp.float32), 'fc2_w': jax.random.normal(ks[8], (128, 1), dtype=jnp.float32) * (1.0 / np.sqrt(128.0)), 'fc2_b': jnp.zeros((1,), jnp.float32)}
        return inp
    _L0_tok_all = _L0_tok_setup()
    _L0_tok_in = {k: v for k, v in _L0_tok_all.items() if k in ('fc0_w', 'fc0_b', 'w1r', 'w1i', 'w2r', 'w2i', 'pw_w', 'pw_b', 'gamma', 'beta', 'fc1_w', 'fc1_b', 'fc2_w', 'fc2_b')}
    del _L0_tok_all

    def _L0_attn_setup():
        import jax, jax.numpy as jnp
        import numpy as np
        B, T, D = (4, 512, 64)
        W_LORA, A_LORA, G_LORA = (64, 64, 128)
        DECAY_SCALE = -0.6065306597126334
        EPS = D * 1e-05

        def _forward(x, x_mix, W_r, W_k, W_v, W_o, A_w, B_w, b_w, A_a, B_a, b_a, A_g, B_g, k_k, k_a, r_k, gn_w, gn_b):
            b, t, d = x.shape
            shifted = jnp.pad(x, ((0, 0), (1, 0), (0, 0)))[:, :-1]
            delta = shifted - x
            xr, xw, xk, xv, xa, xg = [x + delta * x_mix[i] for i in range(6)]
            r = xr @ W_r
            w = DECAY_SCALE * jax.nn.sigmoid(jnp.tanh(xw @ A_w) @ B_w + b_w)
            k = xk @ W_k
            v = xv @ W_v
            a = jax.nn.sigmoid(xa @ A_a @ B_a + b_a)
            g = jax.nn.sigmoid(xg @ A_g) @ B_g
            kk = k * k_k
            kk = kk / jnp.maximum(jnp.linalg.norm(kk, axis=-1, keepdims=True), 1e-12)
            k = k * (1.0 + (a - 1.0) * k_a)
            decay = jnp.exp(w)

            def step(S, inp):
                r_t, dec_t, k_t, v_t, kk_t, a_t = inp
                b_t = kk_t * a_t
                sa = jnp.einsum('bvk,bk->bv', S, -kk_t)
                S = S * dec_t[:, None, :] + sa[:, :, None] * b_t[:, None, :] + v_t[:, :, None] * k_t[:, None, :]
                o_t = jnp.einsum('bvk,bk->bv', S, r_t)
                return (S, o_t)
            tm = lambda z: jnp.swapaxes(z, 0, 1)
            S0 = jnp.zeros((b, d, d), x.dtype)
            _, o = jax.lax.scan(step, S0, (tm(r), tm(decay), tm(k), tm(v), tm(kk), tm(a)))
            o = jnp.swapaxes(o, 0, 1)
            mu = jnp.mean(o, axis=-1, keepdims=True)
            var = jnp.var(o, axis=-1, keepdims=True)
            o = (o - mu) * jax.lax.rsqrt(var + EPS) * gn_w + gn_b
            o = o + jnp.sum(r * k * r_k, axis=-1, keepdims=True) * v
            return o * g @ W_o
        key = jax.random.key(seed)
        ks = jax.random.split(key, 20)
        n = jax.random.normal
        p = {}
        p['x'] = n(ks[0], (B, T, D), jnp.float32)
        p['x_mix'] = n(ks[1], (6, D), jnp.float32) * 0.1
        s = 1.0 / np.sqrt(D).astype(np.float32)
        p['W_r'] = n(ks[2], (D, D), jnp.float32) * s
        p['W_k'] = n(ks[3], (D, D), jnp.float32) * s
        p['W_v'] = n(ks[4], (D, D), jnp.float32) * s
        p['W_o'] = n(ks[5], (D, D), jnp.float32) * s
        p['A_w'] = n(ks[6], (D, W_LORA), jnp.float32) * s
        p['B_w'] = n(ks[7], (W_LORA, D), jnp.float32) / np.sqrt(W_LORA).astype(np.float32)
        p['b_w'] = n(ks[8], (D,), jnp.float32) * 0.5
        p['A_a'] = n(ks[9], (D, A_LORA), jnp.float32) * s
        p['B_a'] = n(ks[10], (A_LORA, D), jnp.float32) / np.sqrt(A_LORA).astype(np.float32)
        p['b_a'] = n(ks[11], (D,), jnp.float32) * 0.1
        p['A_g'] = n(ks[12], (D, G_LORA), jnp.float32) * s
        p['B_g'] = n(ks[13], (G_LORA, D), jnp.float32) / np.sqrt(G_LORA).astype(np.float32)
        p['k_k'] = n(ks[14], (D,), jnp.float32) * 0.5 + 0.85
        p['k_a'] = n(ks[15], (D,), jnp.float32) * 0.1 + 1.0
        p['r_k'] = n(ks[16], (D,), jnp.float32) * 0.1
        p['gn_w'] = jnp.ones((D,), jnp.float32)
        p['gn_b'] = jnp.zeros((D,), jnp.float32)
        return p
    _L0_attn_all = _L0_attn_setup()
    _L0_attn_in = {k: v for k, v in _L0_attn_all.items() if k in ('x_mix', 'W_r', 'W_k', 'W_v', 'W_o', 'A_w', 'B_w', 'b_w', 'A_a', 'B_a', 'b_a', 'A_g', 'B_g', 'k_k', 'k_a', 'r_k', 'gn_w', 'gn_b')}
    del _L0_attn_all

    def _L0_ffn_setup():
        import jax, jax.numpy as jnp
        import numpy as np
        B, A = (1024, 8)
        IN, OUT = (64, 64)
        SH1, SH2 = (64, 128)
        EH1, EH2 = (128, 64)
        E, TOPK = (4, 2)

        def _shared_mlp(x, W1, b1, W2, b2, W3, b3):
            h = jax.nn.relu(x @ W1 + b1)
            h = jax.nn.relu(h @ W2 + b2)
            return h @ W3 + b3

        def _experts_mlp(x, eW1, eb1, eW2, eb2, eW3, eb3):
            h = jax.nn.relu(jnp.einsum('baf,efh->ebah', x, eW1) + eb1[:, None, None, :])
            h = jax.nn.relu(jnp.einsum('ebah,ehg->ebag', h, eW2) + eb2[:, None, None, :])
            o = jnp.einsum('ebag,ego->ebao', h, eW3) + eb3[:, None, None, :]
            return jnp.moveaxis(o, 0, -1)
        key = jax.random.key(seed)
        ks = jax.random.split(key, 16)
        s = 0.05
        return {'x': jax.random.normal(ks[0], (B, A, IN), jnp.float32), 'sW1': jax.random.normal(ks[1], (IN, SH1), jnp.float32) * s, 'sb1': jnp.zeros((SH1,), jnp.float32), 'sW2': jax.random.normal(ks[2], (SH1, SH2), jnp.float32) * s, 'sb2': jnp.zeros((SH2,), jnp.float32), 'sW3': jax.random.normal(ks[3], (SH2, OUT), jnp.float32) * s, 'sb3': jnp.zeros((OUT,), jnp.float32), 'eW1': jax.random.normal(ks[4], (E, IN, EH1), jnp.float32) * s, 'eb1': jnp.zeros((E, EH1), jnp.float32), 'eW2': jax.random.normal(ks[5], (E, EH1, EH2), jnp.float32) * s, 'eb2': jnp.zeros((E, EH2), jnp.float32), 'eW3': jax.random.normal(ks[6], (E, EH2, OUT), jnp.float32) * s, 'eb3': jnp.zeros((E, OUT), jnp.float32), 'gW': jax.random.normal(ks[7], (IN, E), jnp.float32) * s, 'gb': jnp.zeros((E,), jnp.float32)}
    _L0_ffn_all = _L0_ffn_setup()
    _L0_ffn_in = {k: v for k, v in _L0_ffn_all.items() if k in ('sW1', 'sb1', 'sW2', 'sb2', 'sW3', 'sb3', 'eW1', 'eb1', 'eW2', 'eb2', 'eW3', 'eb3', 'gW', 'gb')}
    del _L0_ffn_all
    return {'x': x, 'L0_tok_fc0_w': _L0_tok_in['fc0_w'], 'L0_tok_fc0_b': _L0_tok_in['fc0_b'], 'L0_tok_w1r': _L0_tok_in['w1r'], 'L0_tok_w1i': _L0_tok_in['w1i'], 'L0_tok_w2r': _L0_tok_in['w2r'], 'L0_tok_w2i': _L0_tok_in['w2i'], 'L0_tok_pw_w': _L0_tok_in['pw_w'], 'L0_tok_pw_b': _L0_tok_in['pw_b'], 'L0_tok_gamma': _L0_tok_in['gamma'], 'L0_tok_beta': _L0_tok_in['beta'], 'L0_tok_fc1_w': _L0_tok_in['fc1_w'], 'L0_tok_fc1_b': _L0_tok_in['fc1_b'], 'L0_tok_fc2_w': _L0_tok_in['fc2_w'], 'L0_tok_fc2_b': _L0_tok_in['fc2_b'], 'L0_attn_x_mix': _L0_attn_in['x_mix'], 'L0_attn_W_r': _L0_attn_in['W_r'], 'L0_attn_W_k': _L0_attn_in['W_k'], 'L0_attn_W_v': _L0_attn_in['W_v'], 'L0_attn_W_o': _L0_attn_in['W_o'], 'L0_attn_A_w': _L0_attn_in['A_w'], 'L0_attn_B_w': _L0_attn_in['B_w'], 'L0_attn_b_w': _L0_attn_in['b_w'], 'L0_attn_A_a': _L0_attn_in['A_a'], 'L0_attn_B_a': _L0_attn_in['B_a'], 'L0_attn_b_a': _L0_attn_in['b_a'], 'L0_attn_A_g': _L0_attn_in['A_g'], 'L0_attn_B_g': _L0_attn_in['B_g'], 'L0_attn_k_k': _L0_attn_in['k_k'], 'L0_attn_k_a': _L0_attn_in['k_a'], 'L0_attn_r_k': _L0_attn_in['r_k'], 'L0_attn_gn_w': _L0_attn_in['gn_w'], 'L0_attn_gn_b': _L0_attn_in['gn_b'], 'L0_ffn_sW1': _L0_ffn_in['sW1'], 'L0_ffn_sb1': _L0_ffn_in['sb1'], 'L0_ffn_sW2': _L0_ffn_in['sW2'], 'L0_ffn_sb2': _L0_ffn_in['sb2'], 'L0_ffn_sW3': _L0_ffn_in['sW3'], 'L0_ffn_sb3': _L0_ffn_in['sb3'], 'L0_ffn_eW1': _L0_ffn_in['eW1'], 'L0_ffn_eb1': _L0_ffn_in['eb1'], 'L0_ffn_eW2': _L0_ffn_in['eW2'], 'L0_ffn_eb2': _L0_ffn_in['eb2'], 'L0_ffn_eW3': _L0_ffn_in['eW3'], 'L0_ffn_eb3': _L0_ffn_in['eb3'], 'L0_ffn_gW': _L0_ffn_in['gW'], 'L0_ffn_gb': _L0_ffn_in['gb']}

def reference(x, L0_tok_fc0_w, L0_tok_fc0_b, L0_tok_w1r, L0_tok_w1i, L0_tok_w2r, L0_tok_w2i, L0_tok_pw_w, L0_tok_pw_b, L0_tok_gamma, L0_tok_beta, L0_tok_fc1_w, L0_tok_fc1_b, L0_tok_fc2_w, L0_tok_fc2_b, L0_attn_x_mix, L0_attn_W_r, L0_attn_W_k, L0_attn_W_v, L0_attn_W_o, L0_attn_A_w, L0_attn_B_w, L0_attn_b_w, L0_attn_A_a, L0_attn_B_a, L0_attn_b_a, L0_attn_A_g, L0_attn_B_g, L0_attn_k_k, L0_attn_k_a, L0_attn_r_k, L0_attn_gn_w, L0_attn_gn_b, L0_ffn_sW1, L0_ffn_sb1, L0_ffn_sW2, L0_ffn_sb2, L0_ffn_sW3, L0_ffn_sb3, L0_ffn_eW1, L0_ffn_eb1, L0_ffn_eW2, L0_ffn_eb2, L0_ffn_eW3, L0_ffn_eb3, L0_ffn_gW, L0_ffn_gb):
    import jax
    import jax.numpy as jnp

    def _L0_tok_ref(x, fc0_w, fc0_b, w1r, w1i, w2r, w2i, pw_w, pw_b, gamma, beta, fc1_w, fc1_b, fc2_w, fc2_b):
        import jax, jax.numpy as jnp
        import numpy as np
        M1, M2, WIDTH, LAYERS = (16, 16, 64, 4)
        B, H, W = (16, 64, 64)
        EPS = 1e-05

        def _spectral_conv(h, w1, w2):
            xf = jnp.fft.rfft2(h)
            top = jnp.einsum('bixy,ioxy->boxy', xf[:, :, :M1, :M2], w1)
            bot = jnp.einsum('bixy,ioxy->boxy', xf[:, :, -M1:, :M2], w2)
            of = jnp.zeros(xf.shape, dtype=xf.dtype)
            of = of.at[:, :, :M1, :M2].set(top)
            of = of.at[:, :, -M1:, :M2].set(bot)
            return jnp.fft.irfft2(of, s=(h.shape[-2], h.shape[-1]))
        h = jnp.einsum('bhwi,ic->bhwc', x, fc0_w) + fc0_b
        h = h.transpose(0, 3, 1, 2)
        for l in range(LAYERS):
            sc = _spectral_conv(h, w1r[l] + 1j * w1i[l], w2r[l] + 1j * w2i[l])
            pw = jnp.einsum('bihw,oi->bohw', h, pw_w[l]) + pw_b[l][None, :, None, None]
            y = sc + pw
            mean = y.mean(axis=(0, 2, 3), keepdims=True)
            var = y.var(axis=(0, 2, 3), keepdims=True)
            y = (y - mean) * jax.lax.rsqrt(var + EPS)
            y = y * gamma[l][None, :, None, None] + beta[l][None, :, None, None]
            h = jax.nn.gelu(y, approximate=False)
        h = h.transpose(0, 2, 3, 1)
        h = jax.nn.gelu(h @ fc1_w + fc1_b, approximate=False)
        out = (h @ fc2_w + fc2_b).squeeze(-1)
        return out

    def _L0_attn_ref(x, x_mix, W_r, W_k, W_v, W_o, A_w, B_w, b_w, A_a, B_a, b_a, A_g, B_g, k_k, k_a, r_k, gn_w, gn_b):
        import jax, jax.numpy as jnp
        import numpy as np
        B, T, D = (4, 512, 64)
        W_LORA, A_LORA, G_LORA = (64, 64, 128)
        DECAY_SCALE = -0.6065306597126334
        EPS = D * 1e-05

        def _forward(x, x_mix, W_r, W_k, W_v, W_o, A_w, B_w, b_w, A_a, B_a, b_a, A_g, B_g, k_k, k_a, r_k, gn_w, gn_b):
            b, t, d = x.shape
            shifted = jnp.pad(x, ((0, 0), (1, 0), (0, 0)))[:, :-1]
            delta = shifted - x
            xr, xw, xk, xv, xa, xg = [x + delta * x_mix[i] for i in range(6)]
            r = xr @ W_r
            w = DECAY_SCALE * jax.nn.sigmoid(jnp.tanh(xw @ A_w) @ B_w + b_w)
            k = xk @ W_k
            v = xv @ W_v
            a = jax.nn.sigmoid(xa @ A_a @ B_a + b_a)
            g = jax.nn.sigmoid(xg @ A_g) @ B_g
            kk = k * k_k
            kk = kk / jnp.maximum(jnp.linalg.norm(kk, axis=-1, keepdims=True), 1e-12)
            k = k * (1.0 + (a - 1.0) * k_a)
            decay = jnp.exp(w)

            def step(S, inp):
                r_t, dec_t, k_t, v_t, kk_t, a_t = inp
                b_t = kk_t * a_t
                sa = jnp.einsum('bvk,bk->bv', S, -kk_t)
                S = S * dec_t[:, None, :] + sa[:, :, None] * b_t[:, None, :] + v_t[:, :, None] * k_t[:, None, :]
                o_t = jnp.einsum('bvk,bk->bv', S, r_t)
                return (S, o_t)
            tm = lambda z: jnp.swapaxes(z, 0, 1)
            S0 = jnp.zeros((b, d, d), x.dtype)
            _, o = jax.lax.scan(step, S0, (tm(r), tm(decay), tm(k), tm(v), tm(kk), tm(a)))
            o = jnp.swapaxes(o, 0, 1)
            mu = jnp.mean(o, axis=-1, keepdims=True)
            var = jnp.var(o, axis=-1, keepdims=True)
            o = (o - mu) * jax.lax.rsqrt(var + EPS) * gn_w + gn_b
            o = o + jnp.sum(r * k * r_k, axis=-1, keepdims=True) * v
            return o * g @ W_o
        return _forward(x, x_mix, W_r, W_k, W_v, W_o, A_w, B_w, b_w, A_a, B_a, b_a, A_g, B_g, k_k, k_a, r_k, gn_w, gn_b)

    def _L0_ffn_ref(x, sW1, sb1, sW2, sb2, sW3, sb3, eW1, eb1, eW2, eb2, eW3, eb3, gW, gb):
        import jax, jax.numpy as jnp
        import numpy as np
        B, A = (1024, 8)
        IN, OUT = (64, 64)
        SH1, SH2 = (64, 128)
        EH1, EH2 = (128, 64)
        E, TOPK = (4, 2)

        def _shared_mlp(x, W1, b1, W2, b2, W3, b3):
            h = jax.nn.relu(x @ W1 + b1)
            h = jax.nn.relu(h @ W2 + b2)
            return h @ W3 + b3

        def _experts_mlp(x, eW1, eb1, eW2, eb2, eW3, eb3):
            h = jax.nn.relu(jnp.einsum('baf,efh->ebah', x, eW1) + eb1[:, None, None, :])
            h = jax.nn.relu(jnp.einsum('ebah,ehg->ebag', h, eW2) + eb2[:, None, None, :])
            o = jnp.einsum('ebag,ego->ebao', h, eW3) + eb3[:, None, None, :]
            return jnp.moveaxis(o, 0, -1)
        all_out = _experts_mlp(x, eW1, eb1, eW2, eb2, eW3, eb3)
        shared = _shared_mlp(x, sW1, sb1, sW2, sb2, sW3, sb3)
        gates = jax.nn.softmax(x @ gW + gb, axis=-1)
        topv, topi = jax.lax.top_k(gates, TOPK)
        topw = jax.nn.softmax(topv, axis=-1)
        sel = jnp.take_along_axis(all_out, topi[:, :, None, :], axis=-1)
        gated = jnp.sum(sel * topw[:, :, None, :], axis=-1)
        return shared + gated
    h = _L0_tok_ref(x, L0_tok_fc0_w, L0_tok_fc0_b, L0_tok_w1r, L0_tok_w1i, L0_tok_w2r, L0_tok_w2i, L0_tok_pw_w, L0_tok_pw_b, L0_tok_gamma, L0_tok_beta, L0_tok_fc1_w, L0_tok_fc1_b, L0_tok_fc2_w, L0_tok_fc2_b)
    h = h + _L0_attn_ref(_layernorm(h, axis=-1), L0_attn_x_mix, L0_attn_W_r, L0_attn_W_k, L0_attn_W_v, L0_attn_W_o, L0_attn_A_w, L0_attn_B_w, L0_attn_b_w, L0_attn_A_a, L0_attn_B_a, L0_attn_b_a, L0_attn_A_g, L0_attn_B_g, L0_attn_k_k, L0_attn_k_a, L0_attn_r_k, L0_attn_gn_w, L0_attn_gn_b)
    h = h + _L0_ffn_ref(_layernorm(h, axis=-1), L0_ffn_sW1, L0_ffn_sb1, L0_ffn_sW2, L0_ffn_sb2, L0_ffn_sW3, L0_ffn_sb3, L0_ffn_eW1, L0_ffn_eb1, L0_ffn_eW2, L0_ffn_eb2, L0_ffn_eW3, L0_ffn_eb3, L0_ffn_gW, L0_ffn_gb)
    return h

_drawn_inputs = setup_inputs


def setup_inputs(seed=0):
    import zlib

    import numpy as np

    out = dict(_drawn_inputs(seed))
    spreads = {'L0_tok_fc0_b': (0.0, 0.8),
     'L0_tok_pw_b': (0.0, 0.8),
     'L0_tok_gamma': (1.0, 0.2),
     'L0_tok_beta': (0.0, 0.1),
     'L0_tok_fc1_b': (0.0, 0.1),
     'L0_attn_gn_w': (1.0, 0.2),
     'L0_attn_gn_b': (0.0, 0.1),
     'L0_ffn_sb1': (0.0, 0.563),
     'L0_ffn_sb2': (0.0, 0.1),
     'L0_ffn_sb3': (0.0, 0.1),
     'L0_ffn_eb1': (0.0, 0.8),
     'L0_ffn_eb2': (0.0, 0.408),
     'L0_ffn_eb3': (0.0, 0.1),
     'L0_ffn_gb': (0.0, 0.1)}
    factors = {'L0_tok_w1r': 8.0, 'L0_tok_w1i': 8.0, 'L0_tok_w2r': 6.688, 'L0_tok_w2i': 8.0}
    for name, (base, spread) in spreads.items():
        noise = np.random.default_rng([zlib.crc32(name.encode()), seed]).standard_normal(out[name].shape)
        drawn = base * np.exp(spread * noise) if base else spread * noise
        out[name] = jnp.asarray(drawn.astype(out[name].dtype))
    for name, factor in factors.items():
        out[name] = (out[name] * factor).astype(out[name].dtype)
    return out
```

```python
from contextlib import ExitStack

import numpy as np

import concourse.bass as bass
from concourse import mybir

F32 = mybir.dt.float32
ACT = mybir.ActivationFunctionType
ALU = mybir.AluOpType
AX = mybir.AxisListType

C = 64
HH = WW = 64
HW = HH * WW
M1 = M2 = 16
NX = 2 * M1
LAYERS = 4
HID = 128
EPS = 1e-5
GN_EPS = C * 1e-5
DECAY_SCALE = -0.6065306597126334
E = 4
BANK = 512


def constants():
    out = {}
    y = np.arange(M2)
    w = np.arange(WW)
    h = np.arange(HH)
    x = np.concatenate([np.arange(M1), np.arange(HH - M1, HH)])
    cy = np.cos(2 * np.pi * np.outer(w, y) / WW)
    sy = np.sin(2 * np.pi * np.outer(w, y) / WW)
    cx = np.cos(2 * np.pi * np.outer(h, x) / HH)
    sx = np.sin(2 * np.pi * np.outer(h, x) / HH)
    f = np.zeros((2, WW, 2, M2, 2))
    for p in range(2):
        f[p, :, p, :, 0], f[p, :, p, :, 1] = cy, -sy
    out["col_fwd"] = f.reshape(128, -1)
    f = np.zeros((HH, 2, 2, NX))
    f[:, 0, 0], f[:, 1, 0] = cx, sx
    f[:, 0, 1], f[:, 1, 1] = -sx, cx
    out["row_fwd"] = f.reshape(128, -1)
    f = np.zeros((2, NX, 2, HH, 2))
    f[:, :, 0, :, 0], f[:, :, 1, :, 0] = cx.T, -sx.T
    f[:, :, 0, :, 1], f[:, :, 1, :, 1] = sx.T, cx.T
    out["row_inv"] = f.reshape(128, -1)
    k = np.where(y == 0, 1.0, 2.0)[:, None] / HW
    f = np.zeros((4, M2, 2, 4, WW))
    for r in range(4):
        f[r, :, 0, r], f[r, :, 1, r] = k * cy.T, -k * sy.T
    out["col_inv"] = f.reshape(128, -1)
    out["ident"] = np.eye(128)
    half = np.arange(128) // C
    chan = np.arange(128) % C
    out["pair_mean"] = 0.5 * (chan[:, None] == chan[None, :])
    out["half_mean"] = (half[:, None] == half[None, :]) / C
    out["half_sum"] = 1.0 * (half[:, None] == half[None, :])
    out["cumulate"] = (half[:, None] == half[None, :]) * (chan[:, None] <= chan[None, :])
    s_, t_ = chan[:, None], np.arange(C)[None, :]
    out["before"] = 1.0 * (s_ < t_)
    out["upto"] = 1.0 * (s_ <= t_)
    out["eye"] = 1.0 * (s_ == t_)
    for k in range(6):
        out[f"join{k}"] = ((s_ >> (k + 1)) == (t_ >> (k + 1))) * (((s_ >> k) & 1) == 0) * (((t_ >> k) & 1) == 1)
    out["join0_rows"] = ((s_ >> 1) == (t_ >> 1)) * ((s_ & 1) == 1) * ((t_ & 1) == 0)
    out["earlier"] = np.tile((np.arange(E)[:, None] > np.arange(E)[None, :]).reshape(1, -1), (128, 1))
    f = np.zeros((32, E, 4, 2, C))
    for b in range(2):
        for c in range(4):
            for e in range(E):
                f[c * 8 + b * 4 + e, e, c, b] = 1
    out["spread"] = np.concatenate([f.reshape(32, -1), np.zeros((96, E * 4 * 128))])
    return out


PE_STEPS = """mean1 var1 pr pk pv pw1 pa1 pg1a pg1b pw2 pvt pa2 pg2 w_turn decay_sum kk_sum p_nt p_n p_mt p_ab p_ak p_mv
q1_m x1_m t1_m q2_m x2_m t2_m q3_m x3_m t3_m q4_m x4_m t4_m q5_m t5_m u_m o_m mean2 bonus_m var2 wo mean3 var3
logits s1 s2a s2b s3 gate_turn e1a0 e1b0 e2_0 spread0 e3_0 e1a1 e1b1 e2_1 spread1 e3_1 e1a2 e1b2 e2_2 spread2 e3_2
e1a3 e1b3 e2_3 spread3 e3_3 out_turn""".split()
ACT_STEPS = """square1 sd1 r k0 v tw ta ga gb sw vt sa g wT kk_sq grow shrink grow_before kk_norm neg_mv
Q1 Q2 Q3 Q4 Q5 U o square2 sd2 square3 sd3 hs ha hb gexp topexp gate_rows
ea0 eb0 ec0 eo0 ea1 eb1 ec1 eo1 ea2 eb2 ec2 eo2 ea3 eb3 ec3 eo3 out_rows""".split()
DVE_STEPS = """x centred1 rstd1 xn delta0 delta m_r m_k m_v m_w m_a m_g ga_s gb_s log_decay a kkr ka kp before_decay
kk_floor kk_rec kk b bd kd rd kkd NT n0 X0 xt0 XT0 MT AB AK
N1 X1 XT1 N2 X2 XT2 N3 X3 XT3 N4 X4 XT4 N5 XT5 rk centred2 rstd2 on gn bonus o2 o3 res
centred3 rstd3 y res_s lg gmax gsub gsum grec gate gt ge gd gm gc rank sel tmax tsub tsel tsum trec tgate
w0 y0 w1 y1 w2 y2 w3 y3""".split()


SLOTS = [
    "x",
    "centred log_decay_turned minus_MV h_centred",
    "square rstd sum_before X h_square h_rstd",
    "sd exp_sum X_turned h_sd",
    "xn exp_minus_sum y N_join",
    "delta exp_sum_before shared1 Q",
    "mix_r kk_raw U shared2_0",
    "mix_w kk_square o shared2_1",
    "mix_k kk_norm o_centred sum",
    "mix_v kk o_square o_rstd expert1_0",
    "mix_a k_factor kk_recip o_sd expert1_1",
    "mix_g k_scaled",
    "r expert2",
    "k expert_out",
    "v out_rows",
    "g gate_rows",
    "a weighted",
    "log_decay",
    "v_turned",
    "w_hidden b rk",
    "a_hidden b_decayed o_norm",
    "g_hidden0 k_decayed o_gated",
    "g_hidden1 kk_decayed h",
    "r_decayed bonus",
    "N_turned",
    "M_turned",
    "scores_b",
    "scores_k",
]


class Sem:

    def __init__(self, sem, per, credit):
        self.sem, self.per, self.credit = sem, per, credit

    def at(self, turn, k=None):
        return self.sem, turn * self.per + (self.credit + (self.per if k is None else k))


class DmaSem:

    def __init__(self, sems, dmas, credit):
        self.sems, self.dmas, self.credit = sems, dmas, credit

    def of(self, turn, buf):
        return self.sems[buf], turn * (8 * self.dmas) + (self.credit + 16 * self.dmas - 8 * self.dmas * buf)


def build(nc, B, ins, consts, out, spectra, products, field, x_spectra):
    NP = B // 2
    raised = []
    offs, n = {}, 0
    for name, width in consts["layout"]:
        offs[name] = (n, width)
        n += width
    ctx = ExitStack()
    with ctx:
        def sb(name, shape):
            return ctx.enter_context(nc.sbuf_tensor(name, shape, F32))

        sems = []

        def dma_sem(name, dmas=1, credit=0, owner="sync"):
            s = DmaSem([ctx.enter_context(nc.semaphore(f"{name}{b}")) for b in range(2)], dmas, credit)
            if credit:
                for x in s.sems:
                    sems.append((owner, Sem(x, 0, credit)))
            return s

        def sem(name, per=1, credit=0, owner=None):
            s = Sem(ctx.enter_context(nc.semaphore(name)), per, credit)
            if credit:
                sems.append((owner, s))
            return s

        cst = sb("cst", [128, n])
        cs = {k: cst[:, o:o + wd] for k, (o, wd) in offs.items()}
        arena = sb("arena", [128, 28 * 1024])
        top = [0]

        def area(start, *widths):
            at, got = start, []
            for wd in widths:
                got.append(arena[:, at:at + wd])
                at += wd
            assert at <= 28 * 1024, at
            return got

        a_y1, a_x0, a_x1, a_hT, a_f10, a_f11, a_t2, a_f20, a_f21 = area(0, HW, HW, HW, HW, 2048, 2048, 2048, 1024, 1024)
        a_y0, = area(24 * 1024, HW)
        a_y, a_x, a_f1, a_f2 = [a_y0, a_y1], [a_x0, a_x1], [a_f10, a_f11], [a_f20, a_f21]
        bd0, bd1, bw0, bw1, bo0, bo1 = area(0, B * 64, B * 64, 4096, 4096, 2048, 2048)
        b_d, b_w, b_o = [bd0, bd1], [bw0, bw1], [bo0, bo1]
        c_y0, c_y1, c_of, c_gs, c_gt0, c_gt1, c_o0, c_o1 = area(0, HW, HW, 2048, 2048, 2048, 2048, HW, HW)
        c_y, c_gt, c_o = [c_y0, c_y1], [c_gt0, c_gt1], [c_o0, c_o1]
        f_y0 = a_y0
        f_y1, f_g, f_s0, f_s1, f_s2, f_s3 = area(0, HW, 4 * BANK, BANK, BANK, BANK, BANK)
        f_s = [f_s0, f_s1, f_s2, f_s3]
        f_y = [f_y0, f_y1]
        pw = sb("pw", [128, 2, 128])
        pwb = sb("pwb", [128, LAYERS + 1])
        gamma = sb("gamma", [128, LAYERS])
        beta = sb("beta", [128, LAYERS])
        stats_ax = sb("stats_ax", [128, max(NP * 8 * 6, B // 2 * C)])
        stats = stats_ax[:, 0:NP * 8 * 6].rearrange("p (a b) -> p a b", b=6)
        norm = sb("norm", [128, 2])
        small = sb("small", [128, 16])
        fc0 = sb("fc0", [128, 128])
        fc0b = sb("fc0b", [128, 1])
        fc0_turned = sb("fc0_turned", [128, 128])
        fc0x = sb("fc0x", [128, 128])
        fc1 = sb("fc1", [128, 2, HID])
        fc1b = sb("fc1b", [128, 1])
        fc2 = sb("fc2", [128, HID])
        fc2b = sb("fc2b", [128, 1])
        tok = sb("tok", [128, B, 32])
        eps = sb("eps", [128, 1])
        gn_eps = sb("gn_eps", [128, 1])
        gates = sb("gates", [128, 2, 24, 32])
        bd_names = ["W_r", "W_k", "W_v", "A_w", "B_w", "A_a", "B_a", "W_o", "sW1", "eW3_0", "eW3_1", "eW3_2", "eW3_3"]
        bdw = sb("bdw", [128, len(bd_names), 128])
        bd = {k: bdw[:, i, :] for i, k in enumerate(bd_names)}
        up_names = ["A_g", "sW2", "eW1_0", "eW1_1", "eW1_2", "eW1_3"]
        upw = sb("upw", [128, len(up_names), 128])
        up = {k: upw[:, i, :] for i, k in enumerate(up_names)}
        dn_names = ["B_g", "sW3", "eW2_0", "eW2_1", "eW2_2", "eW2_3"]
        dnw = sb("dnw", [128, len(dn_names), 64])
        dn = {k: dnw[:, i, :] for i, k in enumerate(dn_names)}
        nv = ins["vecs"].shape[1]
        vecs = sb("vecs", [128, nv])
        vec = {k: vecs[:, i:i + 1] for i, k in enumerate(consts["vecs"])}
        gWs = sb("gWs", [128, 2 * E])
        gbs = sb("gbs", [128, E])
        halved = sb("halved", [128, 2])
        zero = sb("zero", [128, 1])

        ps = ctx.enter_context(nc.psum_tensor("ps", [128, 8, BANK], F32))

        sp_turns = ctx.enter_context(nc.semaphore("sp_turns"))
        pe_waits = ctx.enter_context(nc.semaphore("pe_waits"))
        s_const = sem("s_const")
        s_inputs = sem("s_inputs")
        s_weights = sem("s_weights")
        s_zero = sem("s_zero")
        x_done = sem("x_done", 1)
        z_x = dma_sem("z_x", 1, 0)
        z_mm = sem("z_mm", 8, 16, "tensor")
        z_ev = sem("z_ev", 8, 8, "scalar")
        z_st = dma_sem("z_st", 1, 16)
        a_ld = dma_sem("a_ld", 1, 0)
        a_h = sem("a_h", 4)
        a_t1 = sem("a_t1", 8, 16, "tensor")
        a_t1e = sem("a_t1e", 8, 8, "vector")
        a_f1m = sem("a_f1m", 4, 4, "tensor")
        a_f1e = sem("a_f1e", 4, 4, "scalar")
        a_t2m = sem("a_t2m", 4, 8, "tensor")
        a_t2d = sem("a_t2d", 2, 2, "vector")
        a_t2a = sem("a_t2a", 2, 2, "scalar")
        a_f2m = sem("a_f2m", 2, 2, "tensor")
        a_f2e = sem("a_f2e", 2, 2, "vector")
        a_st = dma_sem("a_st", 4, 128)
        b_ld = dma_sem("b_ld", 1, 0)
        b_wl = dma_sem("b_wl", 2, 0)
        b_wn = sem("b_wn", 2, 0)
        b_mm = sem("b_mm", 4, 20, "tensor")
        b_ea = sem("b_ea", 2, 4, "scalar")
        b_ev = sem("b_ev", 2, 4, "vector")
        b_st = dma_sem("b_st", 1, 16)
        c_pw = sem("c_pw", 32)
        c_zero = sem("c_zero", 1)
        k_pe = sem("k_pe", 3)
        k_dve = sem("k_dve", 3)
        c_ld = dma_sem("c_ld", 1, 0)
        c_ofl = dma_sem("c_ofl", 2, 0)
        c_h = sem("c_h", 4)
        c_i1 = sem("c_i1", 4, 8, "tensor")
        c_i1e = sem("c_i1e", 4, 4, "vector")
        c_gtm = sem("c_gtm", 4, 4, "tensor")
        c_gte = sem("c_gte", 4, 4, "vector")
        c_om = sem("c_om", 8, 16, "tensor")
        c_oe = sem("c_oe", 8, 8, "scalar")
        c_bn = sem("c_bn", 8, 16, "vector")
        c_st = dma_sem("c_st", 1, 32)
        n_dve = sem("n_dve", 6)
        n_pe = sem("n_pe", 2)
        n_ab = sem("n_ab", 3)
        n_act = sem("n_act", 1)
        f_h = sem("f_h", 4)
        f_m1 = sem("f_m1", 16)
        f_e1 = sem("f_e1", 16, 16, "scalar")
        f_m2 = sem("f_m2", 16, 16, "tensor")
        f_e2 = sem("f_e2", 16, 16, "vector")
        f_sum = sem("f_sum", 16, 16, "vector")
        f_done = sem("f_done", 1)

        step_sems = {k: ctx.enter_context(nc.semaphore(f"steps_{k}")) for k in ("pe", "act", "dve")}
        step_lists = {"pe": PE_STEPS, "act": ACT_STEPS, "dve": DVE_STEPS}
        step_of = {name: (eng, i) for eng, names in step_lists.items() for i, name in enumerate(names)}
        assert len(step_of) == sum(map(len, step_lists.values()))
        GROUP = min(8, B // 2)
        TURNS = B // 2 // (2 * GROUP)
        ax = stats_ax[:, 0:B // 2 * C]
        tiles = [{name: arena[:, (len(SLOTS) * l + i) * BANK:(len(SLOTS) * l + i + 1) * BANK]
                                    for i, names in enumerate(SLOTS) for name in names.split()} for l in range(2)]
        HALF = [slice(0, 64), slice(64, 128)]
        image_blocks = [(hp, slice(64 * g, 64 * g + 64)) for hp in HALF for g in range(GROUP)]
        STEP_CREDIT = 1
        XT = 4
        assert B * 64 == 2 * HW
        XN = NX // 4 * 2

        def a_base(layer):
            return layer * NP + (XT - NP)
        s_ax = sem("s_ax", 64)
        o_st = dma_sem("o_st", 2, 32)

        def step(name, turn, l):
            which, i = step_of[name]
            return step_sems[which], turn * (2 * len(step_lists[which])) + (2 * i + l + 1 + STEP_CREDIT)

        def turn_over(which, turn):
            return step_sems[which], turn * (2 * len(step_lists[which])) + STEP_CREDIT

        def stepper(which):
            at_step = [0]

            def mark(name, l):
                assert step_lists[which][at_step[0] // 2] == name and at_step[0] % 2 == l, (name, l, step_lists[which][at_step[0] // 2])
                at_step[0] += 1
                return step_sems[which], 1
            return mark

        def credits(eng, name):
            for owner, s in sems:
                if owner == name:
                    eng.sem_inc(s.sem, s.credit)

        A_ORDER = [("t1", 0), ("t1", 1), ("f1p", 3), ("t1", 2), ("f1", 0), ("t1", 3), ("t2p", 0), ("t1", 4),
                   ("t2p", 1), ("f1", 1), ("t1", 5), ("t2p", 2), ("t2p", 3), ("t1", 6), ("f1", 2), ("f2p", 0),
                   ("t1", 7), ("f2p", 1)]
        C_ORDER = [s for n in range(8) for s in (("outp", n), ("i1", n) if n < 4 else ("gt", n - 4))]

        def staggered(eng, count, slot):
            slot(0, 0, False, True)
            with eng.Fori(0, count // 2 - 1) as j:
                for u in (1, 2):
                    slot(2 * j + u, u % 2, True, True)
            slot(count - 1, 1, True, True)
            slot(count, 0, True, False)

        def at(column):
            return slice(column, column + 1) if isinstance(column, int) else bass.ds(column, 1)

        def layer_loop(eng, one):
            one(0, ACT.Identity)
            with eng.Fori(1, LAYERS) as layer:
                one(layer, ACT.Gelu)

        block = ctx.enter_context(nc.Block())
        field_v = field.rearrange("q b c n -> q (b c) n")
        spectra_w = spectra.rearrange("k (r c) (q b) m -> q b c r k m", r=2, b=2)
        w_pairs = {k: ins[k].rearrange("l (k x) c n -> l k c x n", x=2) for k in ("wr", "wi")}
        prod_w = products.rearrange("b x m -> x b m")
        prod_r = products.rearrange("b x (r n) -> b (x r) n", r=2)

        @block.sync
        def _(sp):
            credits(sp, "sync")
            sp.dma_start(cst[:, :], consts["ap"]).then_inc(s_const.sem, 16)
            x_src = [ins["x"].rearrange("b i n -> i b n")[i] for i in range(3)] + [ins["ones"].partition_broadcast(128)]
            for i in range(2):
                sp.dma_start(a_y[i][0:B], x_src[i]).then_inc(a_ld.sems[i], 16)
            sp.wait_ge(*a_h.at(0))
            sp.dma_start(a_y[0][0:B], x_src[2]).then_inc(a_ld.sems[0], 16)
            sp.wait_ge(s_zero.sem, 10)
            loads = [(pwb[64 * b:64 * b + 64, 0:LAYERS], ins["pw_b"]) for b in range(2)]
            loads += [(gamma[64 * b:64 * b + 64, :], ins["gamma"]) for b in range(2)]
            loads += [(beta[64 * b:64 * b + 64, :], ins["beta"]) for b in range(2)]
            loads += [(fc0[3 * b:3 * b + 3, 64 * b:64 * b + 64], ins["fc0_w"]) for b in range(2)]
            loads += [(fc0x[4 * b:4 * b + 3, 64 * b:64 * b + 64], ins["fc0_w"]) for b in range(2)]
            loads += [(fc0x[4 * b + 3:4 * b + 4, 64 * b:64 * b + 64], ins["fc0_b"].rearrange("(a c) -> a c", a=1)) for b in range(2)]
            loads += [(fc0b[64 * b:64 * b + 64, :], ins["fc0_b"].rearrange("(c a) -> c a", a=1)) for b in range(2)]
            loads += [(fc1[64 * b:64 * b + 64, b, :], ins["fc1_w"]) for b in range(2)]
            loads += [(fc1b[:, :], ins["fc1_b"].rearrange("(c a) -> c a", a=1)), (fc2[:, :], ins["fc2_w"].rearrange("c a -> (a c)").partition_broadcast(128))]
            loads += [(fc2b[:, :], ins["fc2_b"].partition_broadcast(128))]
            for dst, src in loads:
                sp.dma_start(dst, src).then_inc(s_inputs.sem, 16)
            raised.append(16 * len(loads))
            for p in range(1, XT + 1):
                if 2 < p + 1 < XT:
                    sp.wait_ge(*a_h.at(p - 1))
                    sp.dma_start(a_y[1 - p % 2], x_src[p + 1]).then_inc(a_ld.sems[1 - p % 2], 16)
                sp.wait_ge(*a_f2e.at(p - 1))
                f2 = a_f2[1 - p % 2][0:B].rearrange("p (r k m) -> p r k m", r=2, m=64)
                for r in range(2):
                    for k in (0, NX // 8):
                        sp.dma_start(x_spectra[k:k + NX // 8, r, p - 1].rearrange("k b m -> b k m"),
                                     f2[:, r, k:k + NX // 8]).then_inc(a_st.sems[1 - p % 2], 16)
            for buf in range(2):
                sp.wait_ge(*a_st.of(XT - 2 + buf, buf))
            sp.wait_ge(*x_done.at(0))
            x_pairs = ins["x"].rearrange("(q b) c n -> q (b c) n", b=2)
            x_halves = x_spectra.rearrange("k r i (q b) m -> k q (r i) (b m)", q=2)
            spectra_halves = spectra.rearrange("k p (q b) m -> k q p (b m)", q=2)

            def start_load(it, buf, src):
                sp.wait_ge(*z_mm.at(it - 2))
                sp.sem_inc(sp_turns, 1)
                sp.dma_start(arena[0:8, buf * HW:buf * HW + HW], src).then_inc(z_x.sems[buf], 16)

            def start_store(it, buf, dst):
                sp.wait_ge(*z_ev.at(it))
                sp.sem_inc(sp_turns, 1)
                o = 2 * HW + buf * HW
                sp.dma_start(dst, arena[:, o:o + HW]).then_inc(z_st.sems[buf], 16)

            for q in range(2):
                start_load(q, q, x_halves[0, q])
            with sp.Fori(0, NX // 4 - 1) as k:
                for q in range(2):
                    start_store(2 * k + q, q, spectra_halves[k, q])
                    start_load(2 * k + (q + 2), q, x_halves[k + 1, q])
            for q in range(2):
                start_store(XN - 2 + q, q, spectra_halves[NX // 4 - 1, q])
            for buf in range(2):
                sp.wait_ge(*z_st.of(XN - 2 + buf, buf))
                sp.sem_inc(sp_turns, 1)

            def one(layer, func):
                base = layer * NP
                if func is ACT.Gelu:
                    first = a_base(layer)
                    def a_load(p, buf):
                        sp.wait_ge(*a_h.at(first + p - 2))
                        sp.sem_inc(sp_turns, 1)
                        sp.dma_start(a_y[buf], field_v[p]).then_inc(a_ld.sems[buf], 16)

                    def a_slot(p, buf, load):
                        it = first + p
                        if load:
                            a_load(p + 2, buf)
                        sp.wait_ge(*a_f2e.at(it - 1))
                        sp.sem_inc(sp_turns, 1)
                        f2 = a_f2[1 - buf].rearrange("p (r k m) -> p r k m", r=2, m=64)
                        for b in range(2):
                            for r in range(2):
                                sp.dma_start(spectra_w[p - 1, b, :, r], f2[64 * b:64 * b + 64, r]).then_inc(a_st.sems[1 - buf], 16)
                    a_load(2, 0)
                    with sp.Fori(0, NP // 2 - 2) as j:
                        a_slot(2 * j + 1, 1, True)
                        a_slot(2 * j + 2, 0, True)
                    a_slot(NP - 3, 1, True)
                    a_slot(NP - 2, 0, False)
                    a_slot(NP - 1, 1, False)
                    a_slot(NP, 0, False)
                xbase = layer * NX
                def load_w(k, buf):
                    sp.wait_ge(*b_mm.at(xbase + 2 * k - 3))
                    sp.sem_inc(sp_turns, 1)
                    wv = b_w[buf].rearrange("p (x r n) -> p x r n", x=2, r=2)
                    sp.dma_start(wv[0:64, :, 0], w_pairs["wr"][layer, k]).then_inc(b_wl.sems[buf], 16)
                    sp.dma_start(wv[0:64, :, 1], w_pairs["wi"][layer, k]).then_inc(b_wl.sems[buf], 16)
                def load_d(k, buf):
                    sp.wait_ge(*b_mm.at(xbase + 4 * k - 5))
                    sp.sem_inc(sp_turns, 1)
                    sp.dma_start(b_d[buf], spectra[k].rearrange("p b m -> p (b m)")).then_inc(b_ld.sems[buf], 16)
                def store(x, buf):
                    sp.wait_ge(*b_ea.at(xbase + x))
                    sp.sem_inc(sp_turns, 1)
                    sp.wait_ge(*b_ev.at(xbase + x))
                    sp.sem_inc(sp_turns, 1)
                    sp.dma_start(prod_w[x], b_o[buf][0:B, :]).then_inc(b_st.sems[buf], 16)
                load_w(0, 0)
                if func is ACT.Gelu:
                    for buf in range(2):
                        sp.wait_ge(*a_st.of(a_base(layer) + NP - 2 + buf, buf))
                        sp.sem_inc(sp_turns, 1)
                load_d(0, 0)
                load_w(1, 1)
                load_d(1, 1)
                with sp.Fori(0, NX // 8 - 1) as j:
                    for v in range(8):
                        store(8 * j + v, v % 2)
                        if v % 2 == 1:
                            load_w(4 * j + v // 2 + 2, v // 2 % 2)
                        if v % 4 == 3:
                            load_d(2 * j + v // 4 + 2, v // 4)
                for v in range(8):
                    store(NX - 8 + v, v % 2)
                    if v in (1, 3):
                        load_w(NX // 2 - 2 + v // 2, v // 2 % 2)
                for b in range(2):
                    sp.wait_ge(*c_om.at(base - 1))
                    sp.sem_inc(sp_turns, 1)
                    sp.dma_start(pw[64 * b:64 * b + 64, 0, 64 * b:64 * b + 64], ins["pw_w"][layer]).then_inc(c_pw.sem, 16)
                def load_y(p, buf):
                    if func is ACT.Identity:
                        sp.dma_start(c_y[buf][0:6], x_pairs[p]).then_inc(c_ld.sems[buf], 16)
                    else:
                        sp.dma_start(c_y[buf], field_v[p]).then_inc(c_ld.sems[buf], 16)
                if func is ACT.Identity:
                    sp.wait_ge(*c_zero.at(0))
                def load_of(p, buf):
                    sp.wait_ge(*c_i1.at(base + p - 2))
                    sp.sem_inc(sp_turns, 1)
                    ofv = c_of.rearrange("p (y b o) -> p b y o", b=2, o=C)
                    for b in range(2):
                        sp.dma_start(ofv[64 * buf:64 * buf + 64, b], prod_r[2 * p + b].rearrange("q (y o) -> q y o", o=C)).then_inc(c_ofl.sems[buf], 16)
                def store_o(p, buf):
                    sp.wait_ge(*c_oe.at(base + p))
                    sp.sem_inc(sp_turns, 1)
                    sp.dma_start(field_v[p], c_o[buf]).then_inc(c_st.sems[buf], 16)
                load_y(0, 0)
                for buf in range(2):
                    sp.wait_ge(*b_st.of(xbase + NX - 2 + buf, buf))
                    sp.sem_inc(sp_turns, 1)
                load_of(0, 0)
                load_of(1, 1)
                load_y(1, 1)
                def c_slot(p, buf, load):
                    if load:
                        load_of(p + 1, 1 - buf)
                        sp.wait_ge(*c_om.at(base + p - 1))
                        sp.sem_inc(sp_turns, 1)
                        load_y(p + 1, 1 - buf)
                    store_o(p - 1, 1 - buf)
                with sp.Fori(0, NP // 2 - 1) as j:
                    c_slot(2 * j + 1, 1, True)
                    c_slot(2 * j + 2, 0, True)
                for buf in range(2):
                    sp.wait_ge(*c_st.of(base + NP - 4 + buf, buf))
                    sp.sem_inc(sp_turns, 1)
                sp.dma_start(a_y[0], field_v[0]).then_inc(a_ld.sems[0], 16)
                c_slot(NP - 1, 1, False)
                sp.wait_ge(*c_om.at(base + NP - 2))
                sp.sem_inc(sp_turns, 1)
                sp.dma_start(a_y[1], field_v[1]).then_inc(a_ld.sems[1], 16)
                c_slot(NP, 0, False)
                for buf in range(2):
                    sp.wait_ge(*c_st.of(base + NP - 2 + buf, buf))
                    sp.sem_inc(sp_turns, 1)
            layer_loop(sp, one)
            with sp.Fori(0, NP // 2 - 1) as j:
                for u in range(2):
                    sp.wait_ge(*f_m1.at(2 * j + u))
                    sp.sem_inc(sp_turns, 1)
                    sp.dma_start(f_y[u], field_v[2 * j + u + 2]).then_inc(a_ld.sems[u], 16)
            loads = []
            for b in range(2):
                loads += [(bd[k][64 * b:64 * b + 64, 64 * b:64 * b + 64], ins[k]) for k in bd_names]
                loads += [(up[k][64 * b:64 * b + 64, :], ins[k]) for k in up_names]
                loads += [(gWs[64 * b:64 * b + 64, E * b:E * b + E], ins["gW"])]
            loads += [(dn[k], ins[k]) for k in dn_names]
            loads += [(vecs[:, :], ins["vecs"]), (gbs[:, :], ins["gb"].partition_broadcast(128))]
            for dst, src in loads:
                sp.dma_start(dst, src).then_inc(s_weights.sem, 16)
            raised.append(16 * len(loads))
            sp.wait_ge(*f_done.at(0))
            axv = ax.rearrange("p (b t) -> p b t", t=C)
            for b in range(2):
                for a in range(2):
                    sp.dma_start(axv[64 * b:64 * b + 64, :, 32 * a:32 * a + 32],
                                 tok[64 * a:64 * a + 64, b * (B // 2):(b + 1) * (B // 2), :]).then_inc(s_ax.sem, 16)
            out_v = out.rearrange("(a g c b) t d -> a g (b t) c d", a=2, c=GROUP // 2, b=2)
            with sp.Fori(0, TURNS) as turn:
                for l in range(2):
                    sp.wait_ge(*step("out_rows", turn, l))
                    sp.sem_inc(sp_turns, 1)
                    rows = tiles[l]["out_rows"].rearrange("p (c a d) -> p c a d", a=2, d=C)
                    for a in range(2):
                        sp.dma_start(out_v[a, 2 * turn + l], rows[:, :, a]).then_inc(o_st.sems[l], 16)
            for l in range(2):
                sp.wait_ge(o_st.sems[l], 32 + 32 * TURNS)

        INPUTS, WEIGHTS = raised

        @block.gpsimd
        def _(pool):
            pool.memset(pw[:, :, :], 0.0).then_inc(s_zero.sem, 1)
            pool.memset(fc0[:, :], 0.0).then_inc(s_zero.sem, 1)
            pool.memset(eps[:, :], EPS).then_inc(s_zero.sem, 1)
            pool.memset(gWs[:, :], 0.0).then_inc(s_zero.sem, 1)
            pool.memset(gn_eps[:, :], GN_EPS).then_inc(s_zero.sem, 1)
            pool.memset(bdw[:, :, :], 0.0).then_inc(s_zero.sem, 1)
            pool.memset(zero[:, :], 0.0).then_inc(s_zero.sem, 1)
            pool.memset(pwb[:, :], 0.0).then_inc(s_zero.sem, 1)
            pool.memset(fc1[:, :, :], 0.0).then_inc(s_zero.sem, 1)
            pool.memset(fc0x[:, :], 0.0).then_inc(s_zero.sem, 1)
            pool.wait_ge(*a_f2e.at(XT - 1))
            pool.memset(arena[:, 0:2 * HW], 0.0).then_inc(x_done.sem, 1)
            def one(layer, func):
                with pool.Fori(0, NX // 4) as j:
                    for v in range(4):
                        wv = b_w[v // 2].rearrange("p (x r n) -> p x r n", x=2, r=2)[:, v % 2]
                        if v % 2 == 0:
                            pool.wait_ge(*b_wl.of(layer * (NX // 2) + 2 * j + v // 2, v // 2))
                        none = zero[0:64, 0:1].to_broadcast([64, M2 * C])
                        pool.tensor_tensor(wv[64:128, 0], none, wv[0:64, 1], ALU.subtract).then_inc(b_wn.sem, 1)
                        pool.tensor_tensor(wv[64:128, 1], none, wv[0:64, 0], ALU.add).then_inc(b_wn.sem, 1)
                if func is ACT.Identity:
                    pool.wait_ge(*b_mm.at(NX - 1))
                    pool.memset(arena[:, 0:2 * HW], 0.0).then_inc(c_zero.sem, 1)
            layer_loop(pool, one)

        @block.tensor
        def _(pe):
            credits(pe, "tensor")
            pe.sem_inc(step_sems["pe"], STEP_CREDIT)
            pe.wait_ge(s_const.sem, 16)
            def a_phase(base, count):
                def slot(p, buf, prev, cur):
                    it = base + p
                    for kind, n in A_ORDER:
                        if kind == "t1" and cur:
                            if n % 2 == 0:
                                pe.wait_ge(*a_h.at(it, n // 2 + 1))
                            pe.wait_ge(*a_t1e.at(it, n - 1))
                            for i in range(4):
                                t = 4 * n + i
                                mm = pe.transpose(ps[:, n % 2, i * 128:i * 128 + 128], a_x[buf][:, t * 128:t * 128 + 128], cs["ident"])
                            mm.then_inc(a_t1.sem, 1)
                        elif (kind == "f1" and cur) or (kind == "f1p" and prev):
                            t0 = it if kind == "f1" else it - 1
                            pe.wait_ge(*a_t1e.at(t0, 2 * n + 2))
                            pe.wait_ge(*a_f1e.at(t0, n - 1))
                            for i in range(8):
                                t = 8 * n + i
                                mm = pe.matmul(ps[:, 2 + n % 2, i * 64:i * 64 + 64], a_hT[:, t * 128:t * 128 + 128],
                                               cs["col_fwd"], start=True, stop=True)
                            mm.then_inc(a_f1m.sem, 1)
                        elif kind == "t2p" and prev:
                            if n == 0:
                                pe.wait_ge(*a_f1e.at(it - 1))
                            pe.wait_ge(*(a_t2d if n % 2 == 0 else a_t2a).at(it - 1, n // 2))
                            for i in range(4):
                                mm = pe.transpose(ps[:, 4 + n % 2, i * 128:i * 128 + 128], a_f1[1 - buf][:, (4 * n + i) * 128:(4 * n + i) * 128 + 128], cs["ident"])
                            mm.then_inc(a_t2m.sem, 1)
                        elif kind == "f2p" and prev:
                            pe.wait_ge(*a_t2d.at(it - 1, n + 1))
                            pe.wait_ge(*a_t2a.at(it - 1, n + 1))
                            pe.wait_ge(*a_f2e.at(it - 2, n + 1))
                            for i in range(8):
                                y = 8 * n + i
                                mm = pe.matmul(ps[:, 6 + n, i * 64:i * 64 + 64], a_t2[:, y * 128:y * 128 + 128],
                                               cs["row_fwd"], start=True, stop=True)
                            mm.then_inc(a_f2m.sem, 1)
                staggered(pe, count, slot)

            a_phase(0, XT)
            pe.wait_ge(*x_done.at(0))
            pe.wait_ge(s_inputs.sem, INPUTS)
            with pe.Fori(0, XN // 2) as j:
                for u in range(2):
                    it = 2 * j + u
                    pe.wait_ge(*z_x.of(it, u))
                    for n in range(8):
                        pe.wait_ge(*z_ev.at(it - 1, n + 1))
                        xt = arena[:, u * HW + n * BANK:u * HW + (n + 1) * BANK]
                        pe.matmul(ps[:, n, :], fc0x[:, :], xt, start=True, stop=True).then_inc(z_mm.sem, 1)

            def b_phase(layer):
                xbase = layer * NX
                with pe.Fori(0, NX // 8) as j:
                    for v in range(8):
                        x = 8 * j + v
                        if v % 4 == 0:
                            pe.wait_ge(*b_ld.of(layer * (NX // 4) + 2 * j + v // 4, v // 4))
                        pe.wait_ge(*b_wn.at(xbase + x))
                        dv = b_d[v // 4].rearrange("p (b x y) -> p x y b", b=B, y=M2)
                        wv = b_w[v // 2 % 2].rearrange("p (x r y o) -> p x y r o", x=2, r=2, o=C)[:, v % 2]
                        for n in range(4):
                            pe.wait_ge(*(b_ev if n % 2 == 0 else b_ea).at(xbase + x - 2, n // 2 + 1))
                            for i in range(4):
                                y = 4 * n + i
                                mm = pe.matmul(ps[0:B, 4 * (v % 2) + n, i * 128:i * 128 + 128], dv[:, v % 4, y],
                                               wv[:, y], start=True, stop=True)
                            mm.then_inc(b_mm.sem, 1)

            def c_phase(base, weights):
                def slot(p, buf, prev, cur):
                    it = base + p
                    for kind, n in C_ORDER:
                        if kind == "outp" and prev:
                            if n % 2 == 0:
                                pe.wait_ge(*c_h.at(it - 1, n // 2 + 1))
                            pe.wait_ge(*c_gte.at(it - 1, n // 2 + 1))
                            pe.wait_ge(*c_oe.at(it - 1, n - 3))
                            bank = 4 + n % 4
                            pe.matmul(ps[:, bank, :], weights, c_y[1 - buf][:, n * BANK:(n + 1) * BANK], start=True, stop=False)
                            for i in range(2):
                                k = 2 * n + i
                                mm = pe.matmul(ps[:, bank, i * 256:i * 256 + 256], c_gt[1 - buf][:, k * 128:k * 128 + 128],
                                               cs["col_inv"], start=False, stop=(i == 1))
                            mm.then_inc(c_om.sem, 1)
                        elif kind == "i1" and cur:
                            if n == 0:
                                pe.wait_ge(*c_ofl.of(it, buf))
                            pe.wait_ge(*c_i1e.at(it, n - 1))
                            for i in range(4):
                                mm = pe.matmul(ps[:, n % 2, i * 128:i * 128 + 128], c_of[64 * buf:64 * buf + 64, (4 * n + i) * 128:(4 * n + i) * 128 + 128],
                                               cs["row_inv"][64 * buf:64 * buf + 64], start=True, stop=True)
                            mm.then_inc(c_i1.sem, 1)
                        elif kind == "gt" and cur:
                            if n == 0:
                                pe.wait_ge(*c_i1e.at(it))
                            pe.wait_ge(*c_gte.at(it, n - 1))
                            for i in range(4):
                                k = 4 * n + i
                                mm = pe.transpose(ps[:, 2 + n % 2, i * 128:i * 128 + 128], c_gs[:, k * 128:k * 128 + 128], cs["ident"])
                            mm.then_inc(c_gtm.sem, 1)
                staggered(pe, NP, slot)

            def one(layer, func):
                if func is ACT.Gelu:
                    a_phase(a_base(layer), NP)
                b_phase(layer)
                pe.wait_ge(*c_pw.at(layer))
                if func is ACT.Identity:
                    pe.wait_ge(*b_ev.at(NX - 1))
                    pe.wait_ge(*b_ea.at(NX - 1))
                    pe.transpose(ps[:, 0, 0:128], fc0[:, :], cs["ident"]).then_inc(k_pe.sem, 1)
                    pe.matmul(ps[:, 2, 0:1], pw[:, 0, :], fc0b[:, 0:1], start=True, stop=True).then_inc(k_pe.sem, 1)
                    pe.wait_ge(*k_dve.at(0, 1))
                    pe.matmul(ps[:, 1, 0:128], fc0_turned[:, :], pw[:, 0, :], start=True, stop=True).then_inc(k_pe.sem, 1)
                    pe.wait_ge(*k_dve.at(0))
                    c_phase(0, pw[:, 1, :])
                else:
                    c_phase(layer * NP, pw[:, 0, :])
                pe.wait_ge(*n_dve.at(layer + 1, 1))
                pe.matmul(ps[:, 0, 0:1], cs["pair_mean"], small[:, 0:1], start=True, stop=True).then_inc(n_pe.sem, 1)
                pe.wait_ge(*n_dve.at(layer + 1, 4))
                pe.matmul(ps[:, 1, 0:1], cs["pair_mean"], small[:, 4:5], start=True, stop=True).then_inc(n_pe.sem, 1)
            layer_loop(pe, one)

            def slot_f(it, buf, prev, cur):
                for n in range(16):
                    if cur:
                        if n == 0:
                            pe.wait_ge(*f_h.at(it))
                        pe.wait_ge(*f_e1.at(it, n - 3))
                        hv = f_y[buf].rearrange("p (a r w) -> p r a w", a=2, w=WW)[:, 4 * (n % 8):4 * (n % 8) + 4]
                        pe.matmul(ps[:, n % 4, :], fc1[:, n // 8, :], hv, start=True, stop=True).then_inc(f_m1.sem, 1)
                    if (prev and n < 2) or (cur and n >= 2):
                        t0, m = (it - 1, n + 14) if n < 2 else (it, n - 2)
                        pe.wait_ge(*f_e1.at(t0, m + 1))
                        pe.wait_ge(*f_e2.at(t0, m - 3))
                        for r in range(4):
                            mm = pe.transpose(ps[:, 4 + m % 4, 128 * r:128 * r + 128],
                                              f_g[:, (m % 4) * BANK + r * 128:(m % 4) * BANK + r * 128 + 128], cs["ident"])
                        mm.then_inc(f_m2.sem, 1)
            staggered(pe, NP, slot_f)

            pe.wait_ge(*s_ax.at(0))
            pe.wait_ge(s_weights.sem, WEIGHTS)
            mark = stepper("pe")
            with pe.Fori(0, TURNS) as turn:
                for l in range(2):
                    t = tiles[l]
                    pe.wait_ge(*step("x", turn, l))
                    pe.matmul(ps[:, 4 * l + 0, :], cs['half_mean'], t["x"], start=True, stop=True).then_inc(*mark("mean1", l))
                for l in range(2):
                    t = tiles[l]
                    pe.wait_ge(*step("square1", turn, l))
                    pe.matmul(ps[:, 4 * l + 1, :], cs['half_mean'], t["square"], start=True, stop=True).then_inc(*mark("var1", l))
                for l in range(2):
                    t = tiles[l]
                    pe.wait_ge(*step("m_r", turn, l))
                    pe.matmul(ps[:, 4 * l + 0, :], bd['W_r'], t["mix_r"], start=True, stop=True).then_inc(*mark("pr", l))
                for l in range(2):
                    t = tiles[l]
                    pe.wait_ge(*step("m_k", turn, l))
                    pe.wait_ge(*step("sd1", turn, l))
                    pe.matmul(ps[:, 4 * l + 1, :], bd['W_k'], t["mix_k"], start=True, stop=True).then_inc(*mark("pk", l))
                for l in range(2):
                    t = tiles[l]
                    pe.wait_ge(*step("m_v", turn, l))
                    pe.matmul(ps[:, 4 * l + 2, :], bd['W_v'], t["mix_v"], start=True, stop=True).then_inc(*mark("pv", l))
                for l in range(2):
                    t = tiles[l]
                    pe.wait_ge(*step("m_w", turn, l))
                    pe.matmul(ps[:, 4 * l + 3, :], bd['A_w'], t["mix_w"], start=True, stop=True).then_inc(*mark("pw1", l))
                for l in range(2):
                    t = tiles[l]
                    pe.wait_ge(*step("m_a", turn, l))
                    pe.wait_ge(*step("r", turn, l))
                    pe.matmul(ps[:, 4 * l + 0, :], bd['A_a'], t["mix_a"], start=True, stop=True).then_inc(*mark("pa1", l))
                for l in range(2):
                    t = tiles[l]
                    pe.wait_ge(*step("m_g", turn, l))
                    pe.wait_ge(*step("k0", turn, l))
                    hp = HALF[0]
                    pe.matmul(ps[:, 4 * l + 1, :], up['A_g'][hp], t["mix_g"][hp], start=True, stop=True).then_inc(*mark("pg1a", l))
                for l in range(2):
                    t = tiles[l]
                    pe.wait_ge(*step("v", turn, l))
                    hp = HALF[1]
                    pe.matmul(ps[:, 4 * l + 2, :], up['A_g'][hp], t["mix_g"][hp], start=True, stop=True).then_inc(*mark("pg1b", l))
                for l in range(2):
                    t = tiles[l]
                    pe.wait_ge(*step("tw", turn, l))
                    pe.matmul(ps[:, 4 * l + 3, :], bd['B_w'], t["w_hidden"], start=True, stop=True).then_inc(*mark("pw2", l))
                for l in range(2):
                    t = tiles[l]
                    pe.wait_ge(*step("ta", turn, l))
                    pe.sem_inc(pe_waits, 1)
                    for hp, col in image_blocks:
                        mm = pe.matmul(ps[hp, 4 * l + 0, col], t["mix_v"][hp, col], bd['W_v'][hp, hp], start=True, stop=True)
                    mm.then_inc(*mark("pvt", l))
                for l in range(2):
                    t = tiles[l]
                    pe.wait_ge(*step("ga", turn, l))
                    pe.matmul(ps[:, 4 * l + 1, :], bd['B_a'], t["a_hidden"], start=True, stop=True).then_inc(*mark("pa2", l))
                for l in range(2):
                    t = tiles[l]
                    pe.wait_ge(*step("gb_s", turn, l))
                    pe.matmul(ps[HALF[0], 4 * l + 2, :], dn['B_g'], t["g_hidden0"], start=True, stop=True)
                    pe.matmul(ps[HALF[1], 4 * l + 2, :], dn['B_g'], t["g_hidden1"], start=True, stop=True).then_inc(*mark("pg2", l))
                for l in range(2):
                    t = tiles[l]
                    pe.wait_ge(*step("log_decay", turn, l))
                    for c in range(4):
                        mm = pe.transpose(ps[:, 4 * l + 3, 128 * c:128 * c + 128], t["log_decay"][:, 128 * c:128 * c + 128], cs["ident"])
                    mm.then_inc(*mark("w_turn", l))
                for l in range(2):
                    t = tiles[l]
                    pe.wait_ge(*step("wT", turn, l))
                    for c in range(4):
                        mm = pe.matmul(ps[:, 4 * l, 128 * c:128 * c + 128], t["log_decay_turned"][:, 128 * c:128 * c + 128], cs['cumulate'], start=True, stop=True)
                    mm.then_inc(*mark('decay_sum', l))
                for l in range(2):
                    t = tiles[l]
                    pe.wait_ge(*step("kk_sq", turn, l))
                    pe.matmul(ps[:, 4 * l + 1, :], cs['half_sum'], t["kk_square"], start=True, stop=True).then_inc(*mark("kk_sum", l))
                for l in range(2):
                    t = tiles[l]
                    pe.wait_ge(*step("kkd", turn, l))
                    pe.sem_inc(pe_waits, 1)
                    for hp, col in image_blocks:
                        mm = pe.matmul(ps[hp, 4 * l + 2, col], t["b_decayed"][hp, col], t["kk_decayed"][hp, col], start=True, stop=True)
                    mm.then_inc(*mark("p_nt", l))
                for l in range(2):
                    t = tiles[l]
                    for hp, col in image_blocks:
                        mm = pe.matmul(ps[hp, 4 * l + 3, col], t["kk_decayed"][hp, col], t["b_decayed"][hp, col], start=True, stop=True)
                    mm.then_inc(*mark("p_n", l))
                for l in range(2):
                    t = tiles[l]
                    pe.wait_ge(*step("grow_before", turn, l))
                    pe.sem_inc(pe_waits, 1)
                    for hp, col in image_blocks:
                        mm = pe.matmul(ps[hp, 4 * l + 0, col], t["k_decayed"][hp, col], t["kk_decayed"][hp, col], start=True, stop=True)
                    mm.then_inc(*mark("p_mt", l))
                for l in range(2):
                    t = tiles[l]
                    pe.wait_ge(*step("kk_norm", turn, l))
                    pe.sem_inc(pe_waits, 1)
                    for hp, col in image_blocks:
                        mm = pe.matmul(ps[hp, 4 * l + 1, col], t["b_decayed"][hp, col], t["r_decayed"][hp, col], start=True, stop=True)
                    mm.then_inc(*mark("p_ab", l))
                for l in range(2):
                    t = tiles[l]
                    pe.wait_ge(*step("NT", turn, l))
                    pe.sem_inc(pe_waits, 1)
                    for hp, col in image_blocks:
                        mm = pe.matmul(ps[hp, 4 * l + 2, col], t["k_decayed"][hp, col], t["r_decayed"][hp, col], start=True, stop=True)
                    mm.then_inc(*mark("p_ak", l))
                for l in range(2):
                    t = tiles[l]
                    pe.wait_ge(*step("MT", turn, l))
                    pe.sem_inc(pe_waits, 1)
                    for hp, col in image_blocks:
                        mm = pe.matmul(ps[hp, 4 * l + 3, col], t["M_turned"][hp, col], t["v_turned"][hp, col], start=True, stop=True)
                    mm.then_inc(*mark("p_mv", l))
                for l in range(2):
                    t = tiles[l]
                    pe.wait_ge(*step("N1", turn, l))
                    pe.sem_inc(pe_waits, 1)
                    for hp, col in image_blocks:
                        mm = pe.matmul(ps[hp, 4 * l + 0, col], t["N_join"][hp, col], t["X"][hp, col], start=True, stop=True)
                    mm.then_inc(*mark("q1_m", l))
                for l in range(2):
                    t = tiles[l]
                    pe.wait_ge(*step("Q1", turn, l))
                    pe.sem_inc(pe_waits, 1)
                    for hp, col in image_blocks:
                        mm = pe.matmul(ps[hp, 4 * l + 1, col], t["X_turned"][hp, col], t["Q"][hp, col], start=True, stop=True)
                    mm.then_inc(*mark("x1_m", l))
                for l in range(2):
                    t = tiles[l]
                    for hp, col in image_blocks:
                        mm = pe.matmul(ps[hp, 4 * l + 2, col], t["Q"][hp, col], t["X_turned"][hp, col], start=True, stop=True)
                    mm.then_inc(*mark("t1_m", l))
                for l in range(2):
                    t = tiles[l]
                    pe.wait_ge(*step("N2", turn, l))
                    pe.sem_inc(pe_waits, 1)
                    for hp, col in image_blocks:
                        mm = pe.matmul(ps[hp, 4 * l + 0, col], t["N_join"][hp, col], t["X"][hp, col], start=True, stop=True)
                    mm.then_inc(*mark("q2_m", l))
                for l in range(2):
                    t = tiles[l]
                    pe.wait_ge(*step("Q2", turn, l))
                    pe.sem_inc(pe_waits, 1)
                    for hp, col in image_blocks:
                        mm = pe.matmul(ps[hp, 4 * l + 1, col], t["X_turned"][hp, col], t["Q"][hp, col], start=True, stop=True)
                    mm.then_inc(*mark("x2_m", l))
                for l in range(2):
                    t = tiles[l]
                    for hp, col in image_blocks:
                        mm = pe.matmul(ps[hp, 4 * l + 2, col], t["Q"][hp, col], t["X_turned"][hp, col], start=True, stop=True)
                    mm.then_inc(*mark("t2_m", l))
                for l in range(2):
                    t = tiles[l]
                    pe.wait_ge(*step("N3", turn, l))
                    pe.sem_inc(pe_waits, 1)
                    for hp, col in image_blocks:
                        mm = pe.matmul(ps[hp, 4 * l + 0, col], t["N_join"][hp, col], t["X"][hp, col], start=True, stop=True)
                    mm.then_inc(*mark("q3_m", l))
                for l in range(2):
                    t = tiles[l]
                    pe.wait_ge(*step("Q3", turn, l))
                    pe.sem_inc(pe_waits, 1)
                    for hp, col in image_blocks:
                        mm = pe.matmul(ps[hp, 4 * l + 1, col], t["X_turned"][hp, col], t["Q"][hp, col], start=True, stop=True)
                    mm.then_inc(*mark("x3_m", l))
                for l in range(2):
                    t = tiles[l]
                    for hp, col in image_blocks:
                        mm = pe.matmul(ps[hp, 4 * l + 2, col], t["Q"][hp, col], t["X_turned"][hp, col], start=True, stop=True)
                    mm.then_inc(*mark("t3_m", l))
                for l in range(2):
                    t = tiles[l]
                    pe.wait_ge(*step("N4", turn, l))
                    pe.sem_inc(pe_waits, 1)
                    for hp, col in image_blocks:
                        mm = pe.matmul(ps[hp, 4 * l + 0, col], t["N_join"][hp, col], t["X"][hp, col], start=True, stop=True)
                    mm.then_inc(*mark("q4_m", l))
                for l in range(2):
                    t = tiles[l]
                    pe.wait_ge(*step("Q4", turn, l))
                    pe.sem_inc(pe_waits, 1)
                    for hp, col in image_blocks:
                        mm = pe.matmul(ps[hp, 4 * l + 1, col], t["X_turned"][hp, col], t["Q"][hp, col], start=True, stop=True)
                    mm.then_inc(*mark("x4_m", l))
                for l in range(2):
                    t = tiles[l]
                    for hp, col in image_blocks:
                        mm = pe.matmul(ps[hp, 4 * l + 2, col], t["Q"][hp, col], t["X_turned"][hp, col], start=True, stop=True)
                    mm.then_inc(*mark("t4_m", l))
                for l in range(2):
                    t = tiles[l]
                    pe.wait_ge(*step("N5", turn, l))
                    pe.sem_inc(pe_waits, 1)
                    for hp, col in image_blocks:
                        mm = pe.matmul(ps[hp, 4 * l + 0, col], t["N_join"][hp, col], t["X"][hp, col], start=True, stop=True)
                    mm.then_inc(*mark("q5_m", l))
                for l in range(2):
                    t = tiles[l]
                    pe.wait_ge(*step("Q5", turn, l))
                    pe.sem_inc(pe_waits, 1)
                    for hp, col in image_blocks:
                        mm = pe.matmul(ps[hp, 4 * l + 2, col], t["Q"][hp, col], t["X_turned"][hp, col], start=True, stop=True)
                    mm.then_inc(*mark("t5_m", l))
                for l in range(2):
                    t = tiles[l]
                    pe.wait_ge(*step("XT5", turn, l))
                    pe.sem_inc(pe_waits, 1)
                    for hp, col in image_blocks:
                        mm = pe.matmul(ps[hp, 4 * l + 3, col], t["X_turned"][hp, col], t["minus_MV"][hp, col], start=True, stop=True)
                    mm.then_inc(*mark("u_m", l))
                for l in range(2):
                    t = tiles[l]
                    pe.wait_ge(*step("U", turn, l))
                    pe.sem_inc(pe_waits, 1)
                    for hp, col in image_blocks:
                        pe.matmul(ps[hp, 4 * l + 0, col], t["U"][hp, col], t["scores_b"][hp, col], start=True, stop=False)
                        mm = pe.matmul(ps[hp, 4 * l + 0, col], t["v_turned"][hp, col], t["scores_k"][hp, col], start=False, stop=True)
                    mm.then_inc(*mark("o_m", l))
                for l in range(2):
                    t = tiles[l]
                    pe.wait_ge(*step("o", turn, l))
                    pe.matmul(ps[:, 4 * l + 1, :], cs['half_mean'], t["o"], start=True, stop=True).then_inc(*mark("mean2", l))
                for l in range(2):
                    t = tiles[l]
                    pe.wait_ge(*step("rk", turn, l))
                    pe.matmul(ps[:, 4 * l + 2, :], cs['half_sum'], t["rk"], start=True, stop=True).then_inc(*mark("bonus_m", l))
                for l in range(2):
                    t = tiles[l]
                    pe.wait_ge(*step("square2", turn, l))
                    pe.matmul(ps[:, 4 * l + 3, :], cs['half_mean'], t["o_square"], start=True, stop=True).then_inc(*mark("var2", l))
                for l in range(2):
                    t = tiles[l]
                    pe.wait_ge(*step("o3", turn, l))
                    pe.matmul(ps[:, 4 * l + 1, :], bd['W_o'], t["o_gated"], start=True, stop=True).then_inc(*mark("wo", l))
                for l in range(2):
                    t = tiles[l]
                    pe.wait_ge(*step("res", turn, l))
                    pe.matmul(ps[:, 4 * l + 0, :], cs['half_mean'], t["h"], start=True, stop=True).then_inc(*mark("mean3", l))
                for l in range(2):
                    t = tiles[l]
                    pe.wait_ge(*step("square3", turn, l))
                    pe.matmul(ps[:, 4 * l + 1, :], cs['half_mean'], t["h_square"], start=True, stop=True).then_inc(*mark("var3", l))
                for l in range(2):
                    t = tiles[l]
                    pe.wait_ge(*step("y", turn, l))
                    for c in range(4):
                        mm = pe.matmul(ps[:, 4 * l + 2, 8 * c:8 * c + 8], t["y"][:, 128 * c:128 * c + 128], gWs[:, :], start=True, stop=True)
                    mm.then_inc(*mark('logits', l))
                for l in range(2):
                    t = tiles[l]
                    pe.matmul(ps[:, 4 * l + 3, :], bd['sW1'], t["y"], start=True, stop=True).then_inc(*mark("s1", l))
                for l in range(2):
                    t = tiles[l]
                    pe.wait_ge(*step("hs", turn, l))
                    hp = HALF[0]
                    pe.matmul(ps[:, 4 * l + 0, :], up['sW2'][hp], t["shared1"][hp], start=True, stop=True).then_inc(*mark("s2a", l))
                for l in range(2):
                    t = tiles[l]
                    hp = HALF[1]
                    pe.matmul(ps[:, 4 * l + 1, :], up['sW2'][hp], t["shared1"][hp], start=True, stop=True).then_inc(*mark("s2b", l))
                for l in range(2):
                    t = tiles[l]
                    pe.wait_ge(*step("hb", turn, l))
                    pe.matmul(ps[HALF[0], 4 * l + 3, :], dn['sW3'], t["shared2_0"], start=True, stop=True)
                    pe.matmul(ps[HALF[1], 4 * l + 3, :], dn['sW3'], t["shared2_1"], start=True, stop=True).then_inc(*mark("s3", l))
                for l in range(2):
                    t = tiles[l]
                    pe.wait_ge(*step("tgate", turn, l))
                    pe.transpose(ps[0:32, 4 * l + 2, 0:128], gates[:, l, 20, :], cs['ident']).then_inc(*mark('gate_turn', l))
                for l in range(2):
                    t = tiles[l]
                    hp = HALF[0]
                    pe.matmul(ps[:, 4 * l + 0, :], up['eW1_0'][hp], t["y"][hp], start=True, stop=True).then_inc(*mark("e1a0", l))
                for l in range(2):
                    t = tiles[l]
                    hp = HALF[1]
                    pe.matmul(ps[:, 4 * l + 1, :], up['eW1_0'][hp], t["y"][hp], start=True, stop=True).then_inc(*mark("e1b0", l))
                for l in range(2):
                    t = tiles[l]
                    pe.wait_ge(*step("eb0", turn, l))
                    pe.matmul(ps[HALF[0], 4 * l + 3, :], dn['eW2_0'], t["expert1_0"], start=True, stop=True)
                    pe.matmul(ps[HALF[1], 4 * l + 3, :], dn['eW2_0'], t["expert1_1"], start=True, stop=True).then_inc(*mark("e2_0", l))
                for l in range(2):
                    t = tiles[l]
                    for c in range(4):
                        o = (0 * 4 + c) * 128
                        mm = pe.matmul(ps[:, 4 * l + 2, 128 * c:128 * c + 128], cs['spread'][0:32, o:o + 128], t["gate_rows"][0:32, 0:128], start=True, stop=True)
                    mm.then_inc(*mark('spread0', l))
                for l in range(2):
                    t = tiles[l]
                    pe.wait_ge(*step("ec0", turn, l))
                    pe.matmul(ps[:, 4 * l + 0, :], bd['eW3_0'], t["expert2"], start=True, stop=True).then_inc(*mark("e3_0", l))
                for l in range(2):
                    t = tiles[l]
                    pe.wait_ge(*step("eo0", turn, l))
                    hp = HALF[0]
                    pe.matmul(ps[:, 4 * l + 0, :], up['eW1_1'][hp], t["y"][hp], start=True, stop=True).then_inc(*mark("e1a1", l))
                for l in range(2):
                    t = tiles[l]
                    hp = HALF[1]
                    pe.matmul(ps[:, 4 * l + 1, :], up['eW1_1'][hp], t["y"][hp], start=True, stop=True).then_inc(*mark("e1b1", l))
                for l in range(2):
                    t = tiles[l]
                    pe.wait_ge(*step("eb1", turn, l))
                    pe.matmul(ps[HALF[0], 4 * l + 3, :], dn['eW2_1'], t["expert1_0"], start=True, stop=True)
                    pe.matmul(ps[HALF[1], 4 * l + 3, :], dn['eW2_1'], t["expert1_1"], start=True, stop=True).then_inc(*mark("e2_1", l))
                for l in range(2):
                    t = tiles[l]
                    pe.wait_ge(*step("w0", turn, l))
                    for c in range(4):
                        o = (1 * 4 + c) * 128
                        mm = pe.matmul(ps[:, 4 * l + 2, 128 * c:128 * c + 128], cs['spread'][0:32, o:o + 128], t["gate_rows"][0:32, 0:128], start=True, stop=True)
                    mm.then_inc(*mark('spread1', l))
                for l in range(2):
                    t = tiles[l]
                    pe.wait_ge(*step("ec1", turn, l))
                    pe.matmul(ps[:, 4 * l + 0, :], bd['eW3_1'], t["expert2"], start=True, stop=True).then_inc(*mark("e3_1", l))
                for l in range(2):
                    t = tiles[l]
                    pe.wait_ge(*step("eo1", turn, l))
                    hp = HALF[0]
                    pe.matmul(ps[:, 4 * l + 0, :], up['eW1_2'][hp], t["y"][hp], start=True, stop=True).then_inc(*mark("e1a2", l))
                for l in range(2):
                    t = tiles[l]
                    hp = HALF[1]
                    pe.matmul(ps[:, 4 * l + 1, :], up['eW1_2'][hp], t["y"][hp], start=True, stop=True).then_inc(*mark("e1b2", l))
                for l in range(2):
                    t = tiles[l]
                    pe.wait_ge(*step("eb2", turn, l))
                    pe.matmul(ps[HALF[0], 4 * l + 3, :], dn['eW2_2'], t["expert1_0"], start=True, stop=True)
                    pe.matmul(ps[HALF[1], 4 * l + 3, :], dn['eW2_2'], t["expert1_1"], start=True, stop=True).then_inc(*mark("e2_2", l))
                for l in range(2):
                    t = tiles[l]
                    pe.wait_ge(*step("w1", turn, l))
                    for c in range(4):
                        o = (2 * 4 + c) * 128
                        mm = pe.matmul(ps[:, 4 * l + 2, 128 * c:128 * c + 128], cs['spread'][0:32, o:o + 128], t["gate_rows"][0:32, 0:128], start=True, stop=True)
                    mm.then_inc(*mark('spread2', l))
                for l in range(2):
                    t = tiles[l]
                    pe.wait_ge(*step("ec2", turn, l))
                    pe.matmul(ps[:, 4 * l + 0, :], bd['eW3_2'], t["expert2"], start=True, stop=True).then_inc(*mark("e3_2", l))
                for l in range(2):
                    t = tiles[l]
                    pe.wait_ge(*step("eo2", turn, l))
                    hp = HALF[0]
                    pe.matmul(ps[:, 4 * l + 0, :], up['eW1_3'][hp], t["y"][hp], start=True, stop=True).then_inc(*mark("e1a3", l))
                for l in range(2):
                    t = tiles[l]
                    hp = HALF[1]
                    pe.matmul(ps[:, 4 * l + 1, :], up['eW1_3'][hp], t["y"][hp], start=True, stop=True).then_inc(*mark("e1b3", l))
                for l in range(2):
                    t = tiles[l]
                    pe.wait_ge(*step("eb3", turn, l))
                    pe.matmul(ps[HALF[0], 4 * l + 3, :], dn['eW2_3'], t["expert1_0"], start=True, stop=True)
                    pe.matmul(ps[HALF[1], 4 * l + 3, :], dn['eW2_3'], t["expert1_1"], start=True, stop=True).then_inc(*mark("e2_3", l))
                for l in range(2):
                    t = tiles[l]
                    pe.wait_ge(*step("w2", turn, l))
                    for c in range(4):
                        o = (3 * 4 + c) * 128
                        mm = pe.matmul(ps[:, 4 * l + 2, 128 * c:128 * c + 128], cs['spread'][0:32, o:o + 128], t["gate_rows"][0:32, 0:128], start=True, stop=True)
                    mm.then_inc(*mark('spread3', l))
                for l in range(2):
                    t = tiles[l]
                    pe.wait_ge(*step("ec3", turn, l))
                    pe.matmul(ps[:, 4 * l + 0, :], bd['eW3_3'], t["expert2"], start=True, stop=True).then_inc(*mark("e3_3", l))
                for l in range(2):
                    t = tiles[l]
                    pe.wait_ge(*step("y3", turn, l))
                    for c in range(4):
                        mm = pe.transpose(ps[:, 4 * l + 1, 128 * c:128 * c + 128], t["sum"][:, 128 * c:128 * c + 128], cs["ident"])
                    mm.then_inc(*mark("out_turn", l))

        @block.scalar
        def _(act):
            credits(act, "scalar")
            act.sem_inc(step_sems["act"], STEP_CREDIT)
            def gelus(s_ld, s_h, y, it, buf, func, which):
                for q in which:
                    if q == 0:
                        act.wait_ge(*s_ld.of(it, buf))
                    v = y[:, q * 1024:(q + 1) * 1024]
                    act.activation(v, v, func, bias=norm[:, 1:2], scale=norm[:, 0:1]).then_inc(s_h.sem, 1)

            def a_gelu(it, buf, func, q):
                if q == 0:
                    act.wait_ge(*a_ld.of(it, buf))
                    act.wait_ge(*a_t1.at(it - 2))
                cols = slice(q * 1024, (q + 1) * 1024)
                act.activation(a_x[buf][:, cols], a_y[buf][:, cols], func, bias=norm[:, 1:2], scale=norm[:, 0:1]).then_inc(a_h.sem, 1)

            def a_phase(first, count, func):
                for q in range(4):
                    a_gelu(first, 0, func, q)
                def a_slot(p, buf, prev, cur, ahead=True):
                    it = first + p
                    for kind, n in A_ORDER:
                        if kind == "t1" and cur and ahead and n % 2 == 1:
                            a_gelu(it + 1, 1 - buf, func, n // 2)
                        if (kind == "f1" and cur) or (kind == "f1p" and prev):
                            t0, bf = (it, buf) if kind == "f1" else (it - 1, 1 - buf)
                            act.wait_ge(*a_f1m.at(t0, n + 1))
                            act.wait_ge(*a_t2m.at(t0 - 2))
                            dst = a_f1[bf].rearrange("p (y h r) -> p h y r", y=M2, r=2)[:, 16 * n:16 * n + 16]
                            act.activation(dst, ps[:, 2 + n % 2, :].rearrange("p (h y r) -> p h y r", h=16, r=2), ACT.Copy).then_inc(a_f1e.sem, 1)
                        elif kind == "t2p" and prev and n % 2 == 1:
                            act.wait_ge(*a_t2m.at(it - 1, n + 1))
                            act.wait_ge(*a_f2m.at(it - 2))
                            act.activation(a_t2[:, n * BANK:(n + 1) * BANK], ps[:, 4 + n % 2, :], ACT.Copy).then_inc(a_t2a.sem, 1)
                a_slot(0, 0, False, True)
                with act.Fori(0, count // 2 - 1) as j:
                    for u in (1, 2):
                        a_slot(2 * j + u, u % 2, True, True)
                a_slot(count - 1, 1, True, True, False)
                a_slot(count, 0, True, False, False)

            act.wait_ge(*n_dve.at(0))
            a_phase(0, XT, ACT.Identity)
            with act.Fori(0, XN // 2) as j:
                for u in range(2):
                    it = 2 * j + u
                    act.wait_ge(*z_st.of(it - 2, u))
                    for n in range(8):
                        act.wait_ge(*z_mm.at(it, n + 1))
                        o = 2 * HW + u * HW + n * BANK
                        act.activation(arena[:, o:o + BANK], ps[:, n, :], ACT.Copy).then_inc(z_ev.sem, 1)

            def one(layer, func):
                base = layer * NP
                xbase = layer * NX
                if func is ACT.Gelu:
                    act.wait_ge(*n_dve.at(layer))
                    a_phase(a_base(layer), NP, func)
                with act.Fori(0, NX // 2) as j:
                    for u in range(2):
                        x = xbase + 2 * j + u
                        ov = b_o[u].rearrange("p (r y o) -> p y r o", r=2, o=C)
                        act.wait_ge(*b_st.of(x - 2, u))
                        for n in (1, 3):
                            act.wait_ge(*b_mm.at(x, n + 1))
                            act.activation(ov[0:B, 4 * n:4 * n + 4],
                                           ps[0:B, 4 * u + n, :].rearrange("p (y r o) -> p y r o", y=4, r=2), ACT.Copy).then_inc(b_ea.sem, 1)
                def c_slot(p, buf, prev, cur):
                    it = base + p
                    for kind, n in C_ORDER:
                        if kind == "outp":
                            if prev:
                                act.wait_ge(*c_om.at(it - 1, n + 1))
                                if n == 0:
                                    act.wait_ge(*c_st.of(it - 3, 1 - buf))
                                    act.wait_ge(*c_bn.at(it - 3))
                                act.activation(c_o[1 - buf][:, n * BANK:(n + 1) * BANK], ps[:, 4 + n % 4, :], ACT.Identity,
                                               bias=layer_bias).then_inc(c_oe.sem, 1)
                            if cur and n >= 4:
                                gelus(c_ld, c_h, c_y[buf], it, buf, func, [n - 4])
                layer_bias = small[:, 8:9]
                if func is ACT.Identity:
                    act.wait_ge(*k_dve.at(0))
                staggered(act, NP, c_slot)
                act.wait_ge(*n_pe.at(layer, 2))
                act.activation(small[:, 5:6], ps[:, 1, 0:1], ACT.Sqrt, bias=eps[:, 0:1]).then_inc(n_act.sem, 1)
            act.wait_ge(s_inputs.sem, INPUTS)
            layer_loop(act, one)
            act.wait_ge(*n_dve.at(LAYERS))
            def turn(it, buf, nxt):
                for n in range(16):
                    act.wait_ge(*f_m1.at(it, n + 1))
                    act.wait_ge(*f_m2.at(it, n - 3))
                    act.activation(f_g[:, (n % 4) * BANK:(n % 4 + 1) * BANK], ps[:, n % 4, :], ACT.Gelu, bias=fc1b[:, 0:1]).then_inc(f_e1.sem, 1)
                    if nxt and n >= 8 and n % 2 == 0:
                        gelus(a_ld, f_h, f_y[1 - buf], a_base(LAYERS) + it + 1, 1 - buf, ACT.Gelu, [(n - 8) // 2])
            gelus(a_ld, f_h, f_y[0], a_base(LAYERS), 0, ACT.Gelu, range(4))
            with act.Fori(0, NP // 2 - 1) as j:
                for u in range(2):
                    turn(2 * j + u, u, True)
            turn(NP - 2, 0, True)
            turn(NP - 1, 1, False)

            act.wait_ge(*s_ax.at(0))
            act.wait_ge(s_weights.sem, WEIGHTS)
            mark = stepper("act")
            with act.Fori(0, TURNS) as turn:
                for l in range(2):
                    t = tiles[l]
                    act.wait_ge(*step("centred1", turn, l))
                    act.activation(t["square"], t["centred"], ACT.Square).then_inc(*mark("square1", l))
                for l in range(2):
                    t = tiles[l]
                    act.wait_ge(*step("var1", turn, l))
                    act.activation(t["sd"], ps[:, 4 * l + 1, :], ACT.Sqrt, bias=eps[:, 0:1]).then_inc(*mark("sd1", l))
                for l in range(2):
                    t = tiles[l]
                    act.wait_ge(*step("pr", turn, l))
                    act.activation(t["r"], ps[:, 4 * l + 0, :], ACT.Copy).then_inc(*mark("r", l))
                for l in range(2):
                    t = tiles[l]
                    act.wait_ge(*step("pk", turn, l))
                    act.activation(t["k"], ps[:, 4 * l + 1, :], ACT.Copy).then_inc(*mark("k0", l))
                for l in range(2):
                    act.wait_ge(o_st.sems[l], 32 * turn + 32)
                for l in range(2):
                    t = tiles[l]
                    act.wait_ge(*step("pv", turn, l))
                    act.activation(t["v"], ps[:, 4 * l + 2, :], ACT.Copy).then_inc(*mark("v", l))
                for l in range(2):
                    t = tiles[l]
                    act.wait_ge(*step("pw1", turn, l))
                    act.activation(t["w_hidden"], ps[:, 4 * l + 3, :], ACT.Tanh).then_inc(*mark("tw", l))
                for l in range(2):
                    t = tiles[l]
                    act.wait_ge(*step("pa1", turn, l))
                    act.activation(t["a_hidden"], ps[:, 4 * l + 0, :], ACT.Copy).then_inc(*mark("ta", l))
                for l in range(2):
                    t = tiles[l]
                    act.wait_ge(*step("pg1a", turn, l))
                    act.activation(t["g_hidden0"], ps[:, 4 * l + 1, :], ACT.Tanh, scale=0.5).then_inc(*mark("ga", l))
                for l in range(2):
                    t = tiles[l]
                    act.wait_ge(*step("pg1b", turn, l))
                    act.activation(t["g_hidden1"], ps[:, 4 * l + 2, :], ACT.Tanh, scale=0.5).then_inc(*mark("gb", l))
                for l in range(2):
                    t = tiles[l]
                    act.wait_ge(*step("pw2", turn, l))
                    act.activation(t["log_decay"], ps[:, 4 * l + 3, :], ACT.Tanh, bias=halved[:, 0:1], scale=0.5).then_inc(*mark("sw", l))
                for l in range(2):
                    t = tiles[l]
                    act.wait_ge(*step("pvt", turn, l))
                    act.activation(t["v_turned"], ps[:, 4 * l + 0, :], ACT.Copy).then_inc(*mark("vt", l))
                for l in range(2):
                    t = tiles[l]
                    act.wait_ge(*step("pa2", turn, l))
                    act.activation(t["a"], ps[:, 4 * l + 1, :], ACT.Tanh, bias=halved[:, 1:2], scale=0.5).then_inc(*mark("sa", l))
                for l in range(2):
                    t = tiles[l]
                    act.wait_ge(*step("pg2", turn, l))
                    act.activation(t["g"], ps[:, 4 * l + 2, :], ACT.Copy).then_inc(*mark("g", l))
                for l in range(2):
                    t = tiles[l]
                    act.wait_ge(*step("w_turn", turn, l))
                    act.activation(t["log_decay_turned"], ps[:, 4 * l + 3, :], ACT.Copy).then_inc(*mark("wT", l))
                for l in range(2):
                    t = tiles[l]
                    act.wait_ge(*step("m_k", turn, l))
                    act.wait_ge(*step("k0", turn, l))
                    act.activation(t["kk_square"], t["k"], ACT.Square, scale=vec['k_k']).then_inc(*mark("kk_sq", l))
                for l in range(2):
                    t = tiles[l]
                    act.wait_ge(*step("decay_sum", turn, l))
                    act.activation(t["exp_sum"], ps[:, 4 * l + 0, :], ACT.Exp).then_inc(*mark("grow", l))
                for l in range(2):
                    t = tiles[l]
                    act.activation(t["exp_minus_sum"], ps[:, 4 * l + 0, :], ACT.Exp, scale=-1.0).then_inc(*mark("shrink", l))
                for l in range(2):
                    t = tiles[l]
                    act.wait_ge(*step("before_decay", turn, l))
                    act.activation(t["exp_sum_before"], t["sum_before"], ACT.Exp).then_inc(*mark("grow_before", l))
                for l in range(2):
                    t = tiles[l]
                    act.wait_ge(*step("kk_sum", turn, l))
                    act.activation(t["kk_norm"], ps[:, 4 * l + 1, :], ACT.Sqrt).then_inc(*mark("kk_norm", l))
                for l in range(2):
                    t = tiles[l]
                    act.wait_ge(*step("p_mv", turn, l))
                    act.activation(t["minus_MV"], ps[:, 4 * l + 3, :], ACT.Copy, scale=-1.0).then_inc(*mark("neg_mv", l))
                for l in range(2):
                    t = tiles[l]
                    act.wait_ge(*step("q1_m", turn, l))
                    act.activation(t["Q"], ps[:, 4 * l + 0, :], ACT.Copy).then_inc(*mark("Q1", l))
                for l in range(2):
                    t = tiles[l]
                    act.wait_ge(*step("q2_m", turn, l))
                    act.activation(t["Q"], ps[:, 4 * l + 0, :], ACT.Copy).then_inc(*mark("Q2", l))
                for l in range(2):
                    t = tiles[l]
                    act.wait_ge(*step("q3_m", turn, l))
                    act.activation(t["Q"], ps[:, 4 * l + 0, :], ACT.Copy).then_inc(*mark("Q3", l))
                for l in range(2):
                    t = tiles[l]
                    act.wait_ge(*step("q4_m", turn, l))
                    act.activation(t["Q"], ps[:, 4 * l + 0, :], ACT.Copy).then_inc(*mark("Q4", l))
                for l in range(2):
                    t = tiles[l]
                    act.wait_ge(*step("q5_m", turn, l))
                    act.activation(t["Q"], ps[:, 4 * l + 0, :], ACT.Copy).then_inc(*mark("Q5", l))
                for l in range(2):
                    t = tiles[l]
                    act.wait_ge(*step("u_m", turn, l))
                    act.activation(t["U"], ps[:, 4 * l + 3, :], ACT.Copy).then_inc(*mark("U", l))
                for l in range(2):
                    t = tiles[l]
                    act.wait_ge(*step("o_m", turn, l))
                    act.activation(t["o"], ps[:, 4 * l + 0, :], ACT.Copy).then_inc(*mark("o", l))
                for l in range(2):
                    t = tiles[l]
                    act.wait_ge(*step("centred2", turn, l))
                    act.activation(t["o_square"], t["o_centred"], ACT.Square).then_inc(*mark("square2", l))
                for l in range(2):
                    t = tiles[l]
                    act.wait_ge(*step("var2", turn, l))
                    act.activation(t["o_sd"], ps[:, 4 * l + 3, :], ACT.Sqrt, bias=gn_eps[:, 0:1]).then_inc(*mark("sd2", l))
                for l in range(2):
                    t = tiles[l]
                    act.wait_ge(*step("centred3", turn, l))
                    act.activation(t["h_square"], t["h_centred"], ACT.Square).then_inc(*mark("square3", l))
                for l in range(2):
                    t = tiles[l]
                    act.wait_ge(*step("var3", turn, l))
                    act.activation(t["h_sd"], ps[:, 4 * l + 1, :], ACT.Sqrt, bias=eps[:, 0:1]).then_inc(*mark("sd3", l))
                for l in range(2):
                    t = tiles[l]
                    act.wait_ge(*step("s1", turn, l))
                    act.activation(t["shared1"], ps[:, 4 * l + 3, :], ACT.Relu, bias=vec['sb1']).then_inc(*mark("hs", l))
                for l in range(2):
                    t = tiles[l]
                    act.wait_ge(*step("s2a", turn, l))
                    act.activation(t["shared2_0"], ps[:, 4 * l + 0, :], ACT.Relu, bias=vec['sb2']).then_inc(*mark("ha", l))
                for l in range(2):
                    t = tiles[l]
                    act.wait_ge(*step("s2b", turn, l))
                    act.activation(t["shared2_1"], ps[:, 4 * l + 1, :], ACT.Relu, bias=vec['sb2']).then_inc(*mark("hb", l))
                for l in range(2):
                    t = tiles[l]
                    act.wait_ge(*step("gsub", turn, l))
                    act.activation(gates[:, l, 2, :], gates[:, l, 1, :], ACT.Exp).then_inc(*mark("gexp", l))
                for l in range(2):
                    t = tiles[l]
                    act.wait_ge(*step("tsub", turn, l))
                    act.activation(gates[:, l, 17, :], gates[:, l, 16, :], ACT.Exp).then_inc(*mark("topexp", l))
                for l in range(2):
                    t = tiles[l]
                    act.wait_ge(*step("gate_turn", turn, l))
                    act.activation(t["gate_rows"][0:32, 0:128], ps[0:32, 4 * l + 2, 0:128], ACT.Copy).then_inc(*mark("gate_rows", l))
                for l in range(2):
                    t = tiles[l]
                    act.wait_ge(*step("e1a0", turn, l))
                    act.activation(t["expert1_0"], ps[:, 4 * l + 0, :], ACT.Relu, bias=vec['eb1_0']).then_inc(*mark("ea0", l))
                for l in range(2):
                    t = tiles[l]
                    act.wait_ge(*step("e1b0", turn, l))
                    act.activation(t["expert1_1"], ps[:, 4 * l + 1, :], ACT.Relu, bias=vec['eb1_0']).then_inc(*mark("eb0", l))
                for l in range(2):
                    t = tiles[l]
                    act.wait_ge(*step("e2_0", turn, l))
                    act.activation(t["expert2"], ps[:, 4 * l + 3, :], ACT.Relu, bias=vec['eb2_0']).then_inc(*mark("ec0", l))
                for l in range(2):
                    t = tiles[l]
                    act.wait_ge(*step("e3_0", turn, l))
                    act.activation(t["expert_out"], ps[:, 4 * l + 0, :], ACT.Identity, bias=vec['eb3_0']).then_inc(*mark("eo0", l))
                for l in range(2):
                    t = tiles[l]
                    act.wait_ge(*step("e1a1", turn, l))
                    act.activation(t["expert1_0"], ps[:, 4 * l + 0, :], ACT.Relu, bias=vec['eb1_1']).then_inc(*mark("ea1", l))
                for l in range(2):
                    t = tiles[l]
                    act.wait_ge(*step("e1b1", turn, l))
                    act.activation(t["expert1_1"], ps[:, 4 * l + 1, :], ACT.Relu, bias=vec['eb1_1']).then_inc(*mark("eb1", l))
                for l in range(2):
                    t = tiles[l]
                    act.wait_ge(*step("e2_1", turn, l))
                    act.activation(t["expert2"], ps[:, 4 * l + 3, :], ACT.Relu, bias=vec['eb2_1']).then_inc(*mark("ec1", l))
                for l in range(2):
                    t = tiles[l]
                    act.wait_ge(*step("e3_1", turn, l))
                    act.activation(t["expert_out"], ps[:, 4 * l + 0, :], ACT.Identity, bias=vec['eb3_1']).then_inc(*mark("eo1", l))
                for l in range(2):
                    t = tiles[l]
                    act.wait_ge(*step("e1a2", turn, l))
                    act.activation(t["expert1_0"], ps[:, 4 * l + 0, :], ACT.Relu, bias=vec['eb1_2']).then_inc(*mark("ea2", l))
                for l in range(2):
                    t = tiles[l]
                    act.wait_ge(*step("e1b2", turn, l))
                    act.activation(t["expert1_1"], ps[:, 4 * l + 1, :], ACT.Relu, bias=vec['eb1_2']).then_inc(*mark("eb2", l))
                for l in range(2):
                    t = tiles[l]
                    act.wait_ge(*step("e2_2", turn, l))
                    act.activation(t["expert2"], ps[:, 4 * l + 3, :], ACT.Relu, bias=vec['eb2_2']).then_inc(*mark("ec2", l))
                for l in range(2):
                    t = tiles[l]
                    act.wait_ge(*step("e3_2", turn, l))
                    act.activation(t["expert_out"], ps[:, 4 * l + 0, :], ACT.Identity, bias=vec['eb3_2']).then_inc(*mark("eo2", l))
                for l in range(2):
                    t = tiles[l]
                    act.wait_ge(*step("e1a3", turn, l))
                    act.activation(t["expert1_0"], ps[:, 4 * l + 0, :], ACT.Relu, bias=vec['eb1_3']).then_inc(*mark("ea3", l))
                for l in range(2):
                    t = tiles[l]
                    act.wait_ge(*step("e1b3", turn, l))
                    act.activation(t["expert1_1"], ps[:, 4 * l + 1, :], ACT.Relu, bias=vec['eb1_3']).then_inc(*mark("eb3", l))
                for l in range(2):
                    t = tiles[l]
                    act.wait_ge(*step("e2_3", turn, l))
                    act.activation(t["expert2"], ps[:, 4 * l + 3, :], ACT.Relu, bias=vec['eb2_3']).then_inc(*mark("ec3", l))
                for l in range(2):
                    t = tiles[l]
                    act.wait_ge(*step("e3_3", turn, l))
                    act.activation(t["expert_out"], ps[:, 4 * l + 0, :], ACT.Identity, bias=vec['eb3_3']).then_inc(*mark("eo3", l))
                for l in range(2):
                    t = tiles[l]
                    act.wait_ge(*step("out_turn", turn, l))
                    act.activation(t["out_rows"], ps[:, 4 * l + 1, :], ACT.Copy).then_inc(*mark('out_rows', l))

        @block.vector
        def _(dve):
            credits(dve, "vector")
            dve.sem_inc(step_sems["dve"], STEP_CREDIT)
            dve.memset(norm[:, 0:1], 1.0).then_inc(n_dve.sem, 1)
            dve.memset(norm[:, 1:2], 0.0).then_inc(n_dve.sem, 5)

            def a_phase(base, count):
                def a_slot(p, buf, prev, cur):
                    it = base + p
                    for kind, n in A_ORDER:
                        if kind == "t1" and cur:
                            dve.wait_ge(*a_t1.at(it, n + 1))
                            if n % 2 == 0:
                                dve.wait_ge(*a_f1m.at(it - 1, n // 2 + 1))
                            dve.tensor_copy(a_hT[:, n * BANK:(n + 1) * BANK], ps[:, n % 2, :]).then_inc(a_t1e.sem, 1)
                        elif kind == "t2p" and prev and n % 2 == 0:
                            dve.wait_ge(*a_t2m.at(it - 1, n + 1))
                            dve.wait_ge(*a_f2m.at(it - 2))
                            dve.tensor_copy(a_t2[:, n * BANK:(n + 1) * BANK], ps[:, 4 + n % 2, :]).then_inc(a_t2d.sem, 1)
                        elif kind == "f2p" and prev:
                            dve.wait_ge(*a_f2m.at(it - 1, n + 1))
                            if n == 0:
                                dve.wait_ge(*a_st.of(it - 3, 1 - buf))
                            dst = a_f2[1 - buf].rearrange("p (q y) -> p y q", y=M2)[:, 8 * n:8 * n + 8]
                            dve.tensor_copy(dst, ps[:, 6 + n, :].rearrange("p (y q) -> p y q", y=8)).then_inc(a_f2e.sem, 1)
                staggered(dve, count, a_slot)

            a_phase(0, XT)

            def one(layer, func):
                base = layer * NP
                xbase = layer * NX
                if func is ACT.Gelu:
                    a_phase(a_base(layer), NP)
                with dve.Fori(0, NX // 2) as j:
                    for u in range(2):
                        x = xbase + 2 * j + u
                        ov = b_o[u].rearrange("p (r y o) -> p y r o", r=2, o=C)
                        dve.wait_ge(*b_st.of(x - 2, u))
                        for n in (0, 2):
                            dve.wait_ge(*b_mm.at(x, n + 1))
                            dve.tensor_copy(ov[0:B, 4 * n:4 * n + 4],
                                            ps[0:B, 4 * u + n, :].rearrange("p (y r o) -> p y r o", y=4, r=2)).then_inc(b_ev.sem, 1)
                if func is ACT.Identity:
                    dve.wait_ge(*k_pe.at(0, 1))
                    dve.tensor_copy(fc0_turned[:, :], ps[:, 0, 0:128]).then_inc(k_dve.sem, 1)
                    dve.wait_ge(*k_pe.at(0, 2))
                    dve.tensor_tensor(small[:, 8:9], pwb[:, 0:1], ps[:, 2, 0:1], ALU.add).then_inc(k_dve.sem, 1)
                    dve.wait_ge(*k_pe.at(0, 3))
                    dve.tensor_copy(pw[:, 1, :], ps[:, 1, 0:128]).then_inc(k_dve.sem, 1)
                def c_slot(p, buf, prev, cur):
                    it = base + p
                    for kind, n in C_ORDER:
                        if kind == "i1" and cur:
                            dve.wait_ge(*c_i1.at(it, n + 1))
                            dve.wait_ge(*c_gtm.at(it - 1))
                            dst = c_gs.rearrange("p (h y r) -> p y h r", h=HH, r=2)[:, 4 * n:4 * n + 4]
                            dve.tensor_copy(dst, ps[:, n % 2, :].rearrange("p (y h r) -> p y h r", y=4, r=2)).then_inc(c_i1e.sem, 1)
                        elif kind == "gt" and cur:
                            dve.wait_ge(*c_gtm.at(it, n + 1))
                            dve.wait_ge(*c_om.at(it - 2))
                            dve.tensor_copy(c_gt[buf][:, n * BANK:(n + 1) * BANK], ps[:, 2 + n % 2, :]).then_inc(c_gte.sem, 1)
                        elif kind == "outp" and prev:
                            dve.wait_ge(*c_oe.at(it - 1, n + 1))
                            dve.bn_stats(stats[:, (p - 1) * 8 + n, :], c_o[1 - buf][:, n * BANK:(n + 1) * BANK]).then_inc(c_bn.sem, 1)
                staggered(dve, NP, c_slot)
                dve.wait_ge(*c_bn.at(base + NP - 1))
                dve.tensor_copy(small[:, 8:9], pwb[:, at(layer + 1)]).then_inc(n_ab.sem, 1)
                dve.bn_aggr(small[:, 0:2], stats[:, :, :].rearrange("p a b -> p (a b)")).then_inc(n_dve.sem, 1)
                dve.wait_ge(*n_dve.at(layer + 1, 1))
                dve.wait_ge(*n_pe.at(layer, 1))
                dve.tensor_tensor(small[:, 2:3], small[:, 0:1], ps[:, 0, 0:1], ALU.subtract).then_inc(n_dve.sem, 1)
                dve.wait_ge(*n_dve.at(layer + 1, 2))
                dve.tensor_tensor(small[:, 3:4], small[:, 2:3], small[:, 2:3], ALU.mult).then_inc(n_dve.sem, 1)
                dve.wait_ge(*n_dve.at(layer + 1, 3))
                dve.tensor_tensor(small[:, 4:5], small[:, 3:4], small[:, 1:2], ALU.add).then_inc(n_dve.sem, 1)
                dve.wait_ge(*n_act.at(layer))
                dve.reciprocal(small[:, 6:7], small[:, 5:6]).then_inc(n_dve.sem, 1)
                dve.wait_ge(*n_dve.at(layer + 1, 5))
                dve.tensor_tensor(norm[:, 0:1], small[:, 6:7], gamma[:, at(layer)], ALU.mult).then_inc(n_ab.sem, 1)
                dve.wait_ge(*n_ab.at(layer, 2))
                dve.tensor_tensor(small[:, 7:8], norm[:, 0:1], ps[:, 0, 0:1], ALU.mult).then_inc(n_ab.sem, 1)
                dve.wait_ge(*n_ab.at(layer, 3))
                dve.tensor_tensor(norm[:, 1:2], beta[:, at(layer)], small[:, 7:8], ALU.subtract).then_inc(n_dve.sem, 1)
            dve.wait_ge(s_inputs.sem, INPUTS)
            layer_loop(dve, one)
            tv = tok[:, :, :].rearrange("p (q b) (n r) -> p q (b n) r", b=2, r=4)
            with dve.Fori(0, NP) as it:
                for n in range(17):
                    if n < 16:
                        dve.wait_ge(*f_m2.at(it, n + 1))
                        dve.wait_ge(*f_sum.at(it, n - 3))
                        dve.tensor_tensor(f_s[n % 4].rearrange("p (r c) -> p r c", r=4),
                                          ps[:, 4 + n % 4, :].rearrange("p (r c) -> p r c", r=4),
                                          fc2[:, :].rearrange("p (r c) -> p r c", r=1).to_broadcast([128, 4, HID]), ALU.mult).then_inc(f_e2.sem, 1)
                    if n >= 1:
                        dve.wait_ge(*f_e2.at(it, n))
                        dve.tensor_reduce(tv[:, it, n - 1], f_s[(n - 1) % 4].rearrange("p (r c) -> p r c", r=4), AX.X, ALU.add).then_inc(f_sum.sem, 1)
            dve.wait_ge(*f_sum.at(NP - 1))
            dve.tensor_scalar(tok[:, :, :], tok[:, :, :], fc2b[:, 0:1], None, ALU.add).then_inc(f_done.sem, 1)

            dve.wait_ge(*s_ax.at(0))
            dve.wait_ge(s_weights.sem, WEIGHTS)
            dve.tensor_scalar(halved[:, 0:1], vec["b_w"], 0.5, None, ALU.mult)
            dve.tensor_scalar(halved[:, 1:2], vec["b_a"], 0.5, None, ALU.mult)
            mark = stepper("dve")

            def tt(o, i0, i1, op):
                return dve.tensor_tensor(o, i0, i1, op)

            def img(ap):
                return ap.rearrange("p (g t) -> p g t", t=C)

            def masked(ap):
                return ap.rearrange("p (o t) -> p o t", o=1).to_broadcast([128, GROUP, C])

            with dve.Fori(0, TURNS) as turn:
                P = lambda l, bank: ps[:, 4 * l + bank, :]
                def img(ap):
                    return ap.rearrange('p (g t) -> p g t', t=C)
                def masked(ap):
                    return ap.rearrange('p (o t) -> p o t', o=1).to_broadcast([128, GROUP, C])
                dve.wait_ge(*turn_over("pe", turn))
                dve.wait_ge(*turn_over("act", turn))
                dve.wait_ge(*turn_over("dve", turn))
                for l in range(2):
                    t = tiles[l]
                    dve.tensor_scalar(t["x"], ax[:, bass.ds((2 * turn + l) * BANK, BANK)], 1.0, None, ALU.mult).then_inc(*mark('x', l))
                for l in range(2):
                    t = tiles[l]
                    dve.wait_ge(*step("mean1", turn, l))
                    dve.wait_ge(*step("x", turn, l))
                    tt(t["centred"], t["x"], P(l, 0), ALU.subtract).then_inc(*mark("centred1", l))
                for l in range(2):
                    t = tiles[l]
                    dve.wait_ge(*step("sd1", turn, l))
                    dve.reciprocal(t["rstd"], t["sd"]).then_inc(*mark("rstd1", l))
                for l in range(2):
                    t = tiles[l]
                    dve.wait_ge(*step("rstd1", turn, l))
                    tt(t["xn"], t["centred"], t["rstd"], ALU.mult).then_inc(*mark("xn", l))
                for l in range(2):
                    t = tiles[l]
                    dve.wait_ge(*step("xn", turn, l))
                    dve.tensor_scalar(img(t["delta"])[:, :, 0:1], img(t["xn"])[:, :, 0:1], -1.0, None, ALU.mult).then_inc(*mark("delta0", l))
                for l in range(2):
                    t = tiles[l]
                    tt(img(t["delta"])[:, :, 1:C], img(t["xn"])[:, :, 0:C - 1], img(t["xn"])[:, :, 1:C], ALU.subtract).then_inc(*mark("delta", l))
                for l in range(2):
                    t = tiles[l]
                    dve.wait_ge(*step("delta", turn, l))
                    dve.scalar_tensor_tensor(out=t["mix_r"], in0=t["delta"], scalar=vec['mix0'], in1=t["xn"], op0=ALU.mult, op1=ALU.add).then_inc(*mark("m_r", l))
                for l in range(2):
                    t = tiles[l]
                    dve.scalar_tensor_tensor(out=t["mix_k"], in0=t["delta"], scalar=vec['mix2'], in1=t["xn"], op0=ALU.mult, op1=ALU.add).then_inc(*mark("m_k", l))
                for l in range(2):
                    t = tiles[l]
                    dve.scalar_tensor_tensor(out=t["mix_v"], in0=t["delta"], scalar=vec['mix3'], in1=t["xn"], op0=ALU.mult, op1=ALU.add).then_inc(*mark("m_v", l))
                for l in range(2):
                    t = tiles[l]
                    dve.scalar_tensor_tensor(out=t["mix_w"], in0=t["delta"], scalar=vec['mix1'], in1=t["xn"], op0=ALU.mult, op1=ALU.add).then_inc(*mark("m_w", l))
                for l in range(2):
                    t = tiles[l]
                    dve.scalar_tensor_tensor(out=t["mix_a"], in0=t["delta"], scalar=vec['mix4'], in1=t["xn"], op0=ALU.mult, op1=ALU.add).then_inc(*mark("m_a", l))
                for l in range(2):
                    t = tiles[l]
                    dve.scalar_tensor_tensor(out=t["mix_g"], in0=t["delta"], scalar=vec['mix5'], in1=t["xn"], op0=ALU.mult, op1=ALU.add).then_inc(*mark("m_g", l))
                for l in range(2):
                    t = tiles[l]
                    dve.wait_ge(*step("ga", turn, l))
                    dve.tensor_scalar(t["g_hidden0"], t["g_hidden0"], 0.5, 0.5, ALU.mult, ALU.add).then_inc(*mark("ga_s", l))
                for l in range(2):
                    t = tiles[l]
                    dve.wait_ge(*step("gb", turn, l))
                    dve.tensor_scalar(t["g_hidden1"], t["g_hidden1"], 0.5, 0.5, ALU.mult, ALU.add).then_inc(*mark("gb_s", l))
                for l in range(2):
                    t = tiles[l]
                    dve.wait_ge(*step("sw", turn, l))
                    dve.tensor_scalar(t["log_decay"], t["log_decay"], 0.5 * DECAY_SCALE, 0.5 * DECAY_SCALE, ALU.mult, ALU.add).then_inc(*mark("log_decay", l))
                for l in range(2):
                    t = tiles[l]
                    dve.wait_ge(*step("sa", turn, l))
                    dve.tensor_scalar(t["a"], t["a"], 0.5, 0.5, ALU.mult, ALU.add).then_inc(*mark("a", l))
                for l in range(2):
                    t = tiles[l]
                    dve.wait_ge(*step("pr", turn, l))
                    dve.tensor_scalar(t["kk_raw"], t["k"], vec['k_k'], None, ALU.mult).then_inc(*mark("kkr", l))
                for l in range(2):
                    t = tiles[l]
                    dve.wait_ge(*step("a", turn, l))
                    dve.wait_ge(*step("pa1", turn, l))
                    dve.tensor_scalar(t["k_factor"], t["a"], -1.0, vec['k_a'], ALU.add, ALU.mult).then_inc(*mark("ka", l))
                for l in range(2):
                    t = tiles[l]
                    dve.wait_ge(*step("ka", turn, l))
                    dve.wait_ge(*step("pg1b", turn, l))
                    dve.scalar_tensor_tensor(out=t["k_scaled"], in0=t["k_factor"], scalar=1.0, in1=t["k"], op0=ALU.add, op1=ALU.mult).then_inc(*mark("kp", l))
                for l in range(2):
                    t = tiles[l]
                    dve.wait_ge(*step("decay_sum", turn, l))
                    dve.wait_ge(*step("shrink", turn, l))
                    tt(t["sum_before"], P(l, 0), t["log_decay"], ALU.subtract).then_inc(*mark("before_decay", l))
                for l in range(2):
                    t = tiles[l]
                    dve.wait_ge(*step("kk_norm", turn, l))
                    dve.tensor_scalar(t["kk_norm"], t["kk_norm"], 1e-12, None, ALU.max).then_inc(*mark("kk_floor", l))
                for l in range(2):
                    t = tiles[l]
                    dve.wait_ge(*step("kk_floor", turn, l))
                    dve.reciprocal(t["kk_recip"], t["kk_norm"]).then_inc(*mark("kk_rec", l))
                for l in range(2):
                    t = tiles[l]
                    dve.wait_ge(*step("kk_rec", turn, l))
                    tt(t["kk"], t["kk_raw"], t["kk_recip"], ALU.mult).then_inc(*mark("kk", l))
                for l in range(2):
                    t = tiles[l]
                    dve.wait_ge(*step("kk", turn, l))
                    tt(t["b"], t["kk"], t["a"], ALU.mult).then_inc(*mark("b", l))
                for l in range(2):
                    t = tiles[l]
                    dve.wait_ge(*step("b", turn, l))
                    tt(t["b_decayed"], t["b"], t["exp_minus_sum"], ALU.mult).then_inc(*mark("bd", l))
                for l in range(2):
                    t = tiles[l]
                    tt(t["k_decayed"], t["k_scaled"], t["exp_minus_sum"], ALU.mult).then_inc(*mark("kd", l))
                for l in range(2):
                    t = tiles[l]
                    tt(t["r_decayed"], t["r"], t["exp_sum"], ALU.mult).then_inc(*mark("rd", l))
                for l in range(2):
                    t = tiles[l]
                    tt(t["kk_decayed"], t["kk"], t["exp_sum_before"], ALU.mult).then_inc(*mark("kkd", l))
                for l in range(2):
                    t = tiles[l]
                    dve.wait_ge(*step("p_nt", turn, l))
                    tt(img(t["N_turned"]), img(ps[:, 4 * l + 2, :]), masked(cs["before"]), ALU.mult).then_inc(*mark("NT", l))
                for l in range(2):
                    t = tiles[l]
                    dve.wait_ge(*step("p_n", turn, l))
                    tt(img(t["X"]), img(ps[:, 4 * l + 3, :]), masked(cs["join0_rows"]), ALU.mult).then_inc(*mark("n0", l))
                for l in range(2):
                    t = tiles[l]
                    dve.wait_ge(*step("n0", turn, l))
                    tt(img(t["X"]), masked(cs['eye']), img(t["X"]), ALU.subtract).then_inc(*mark("X0", l))
                for l in range(2):
                    t = tiles[l]
                    tt(img(t["X_turned"]), img(t["N_turned"]), masked(cs['join0']), ALU.mult).then_inc(*mark("xt0", l))
                for l in range(2):
                    t = tiles[l]
                    dve.wait_ge(*step("xt0", turn, l))
                    tt(img(t["X_turned"]), masked(cs['eye']), img(t["X_turned"]), ALU.subtract).then_inc(*mark("XT0", l))
                for l in range(2):
                    t = tiles[l]
                    dve.wait_ge(*step("p_mt", turn, l))
                    tt(img(t["M_turned"]), img(ps[:, 4 * l + 0, :]), masked(cs["before"]), ALU.mult).then_inc(*mark("MT", l))
                for l in range(2):
                    t = tiles[l]
                    dve.wait_ge(*step("p_ab", turn, l))
                    tt(img(t["scores_b"]), img(ps[:, 4 * l + 1, :]), masked(cs["upto"]), ALU.mult).then_inc(*mark("AB", l))
                for l in range(2):
                    t = tiles[l]
                    dve.wait_ge(*step("p_ak", turn, l))
                    tt(img(t["scores_k"]), img(ps[:, 4 * l + 2, :]), masked(cs["upto"]), ALU.mult).then_inc(*mark("AK", l))
                for l in range(2):
                    t = tiles[l]
                    tt(img(t["N_join"]), img(t["N_turned"]), masked(cs['join1']), ALU.mult).then_inc(*mark("N1", l))
                for l in range(2):
                    t = tiles[l]
                    dve.wait_ge(*step("x1_m", turn, l))
                    tt(t["X"], t["X"], P(l, 1), ALU.subtract).then_inc(*mark("X1", l))
                for l in range(2):
                    t = tiles[l]
                    dve.wait_ge(*step("t1_m", turn, l))
                    tt(t["X_turned"], t["X_turned"], P(l, 2), ALU.subtract).then_inc(*mark("XT1", l))
                for l in range(2):
                    t = tiles[l]
                    tt(img(t["N_join"]), img(t["N_turned"]), masked(cs['join2']), ALU.mult).then_inc(*mark("N2", l))
                for l in range(2):
                    t = tiles[l]
                    dve.wait_ge(*step("x2_m", turn, l))
                    tt(t["X"], t["X"], P(l, 1), ALU.subtract).then_inc(*mark("X2", l))
                for l in range(2):
                    t = tiles[l]
                    dve.wait_ge(*step("t2_m", turn, l))
                    tt(t["X_turned"], t["X_turned"], P(l, 2), ALU.subtract).then_inc(*mark("XT2", l))
                for l in range(2):
                    t = tiles[l]
                    tt(img(t["N_join"]), img(t["N_turned"]), masked(cs['join3']), ALU.mult).then_inc(*mark("N3", l))
                for l in range(2):
                    t = tiles[l]
                    dve.wait_ge(*step("x3_m", turn, l))
                    tt(t["X"], t["X"], P(l, 1), ALU.subtract).then_inc(*mark("X3", l))
                for l in range(2):
                    t = tiles[l]
                    dve.wait_ge(*step("t3_m", turn, l))
                    tt(t["X_turned"], t["X_turned"], P(l, 2), ALU.subtract).then_inc(*mark("XT3", l))
                for l in range(2):
                    t = tiles[l]
                    tt(img(t["N_join"]), img(t["N_turned"]), masked(cs['join4']), ALU.mult).then_inc(*mark("N4", l))
                for l in range(2):
                    t = tiles[l]
                    dve.wait_ge(*step("x4_m", turn, l))
                    tt(t["X"], t["X"], P(l, 1), ALU.subtract).then_inc(*mark("X4", l))
                for l in range(2):
                    t = tiles[l]
                    dve.wait_ge(*step("t4_m", turn, l))
                    tt(t["X_turned"], t["X_turned"], P(l, 2), ALU.subtract).then_inc(*mark("XT4", l))
                for l in range(2):
                    t = tiles[l]
                    tt(img(t["N_join"]), img(t["N_turned"]), masked(cs['join5']), ALU.mult).then_inc(*mark("N5", l))
                for l in range(2):
                    t = tiles[l]
                    dve.wait_ge(*step("t5_m", turn, l))
                    tt(t["X_turned"], t["X_turned"], P(l, 2), ALU.subtract).then_inc(*mark("XT5", l))
                for l in range(2):
                    t = tiles[l]
                    dve.scalar_tensor_tensor(out=t["rk"], in0=t["r"], scalar=vec['r_k'], in1=t["k_scaled"], op0=ALU.mult, op1=ALU.mult).then_inc(*mark("rk", l))
                for l in range(2):
                    t = tiles[l]
                    dve.wait_ge(*step("mean2", turn, l))
                    dve.wait_ge(*step("o", turn, l))
                    tt(t["o_centred"], t["o"], P(l, 1), ALU.subtract).then_inc(*mark("centred2", l))
                for l in range(2):
                    t = tiles[l]
                    dve.wait_ge(*step("sd2", turn, l))
                    dve.reciprocal(t["o_rstd"], t["o_sd"]).then_inc(*mark("rstd2", l))
                for l in range(2):
                    t = tiles[l]
                    dve.wait_ge(*step("rstd2", turn, l))
                    tt(t["o_norm"], t["o_centred"], t["o_rstd"], ALU.mult).then_inc(*mark("on", l))
                for l in range(2):
                    t = tiles[l]
                    dve.wait_ge(*step("on", turn, l))
                    dve.tensor_scalar(t["o_norm"], t["o_norm"], vec['gn_w'], vec['gn_b'], ALU.mult, ALU.add).then_inc(*mark("gn", l))
                for l in range(2):
                    t = tiles[l]
                    dve.wait_ge(*step("bonus_m", turn, l))
                    tt(t["bonus"], t["v"], P(l, 2), ALU.mult).then_inc(*mark("bonus", l))
                for l in range(2):
                    t = tiles[l]
                    dve.wait_ge(*step("bonus", turn, l))
                    tt(t["o_norm"], t["o_norm"], t["bonus"], ALU.add).then_inc(*mark("o2", l))
                for l in range(2):
                    t = tiles[l]
                    dve.wait_ge(*step("o2", turn, l))
                    tt(t["o_gated"], t["o_norm"], t["g"], ALU.mult).then_inc(*mark("o3", l))
                for l in range(2):
                    t = tiles[l]
                    dve.wait_ge(*step("wo", turn, l))
                    tt(t["h"], t["x"], P(l, 1), ALU.add).then_inc(*mark("res", l))
                for l in range(2):
                    t = tiles[l]
                    dve.wait_ge(*step("mean3", turn, l))
                    dve.wait_ge(*step("res", turn, l))
                    tt(t["h_centred"], t["h"], P(l, 0), ALU.subtract).then_inc(*mark("centred3", l))
                for l in range(2):
                    t = tiles[l]
                    dve.wait_ge(*step("sd3", turn, l))
                    dve.reciprocal(t["h_rstd"], t["h_sd"]).then_inc(*mark("rstd3", l))
                for l in range(2):
                    t = tiles[l]
                    dve.wait_ge(*step("rstd3", turn, l))
                    tt(t["y"], t["h_centred"], t["h_rstd"], ALU.mult).then_inc(*mark("y", l))
                for l in range(2):
                    t = tiles[l]
                    dve.wait_ge(*step("s3", turn, l))
                    dve.scalar_tensor_tensor(out=t["sum"], in0=P(l, 3), scalar=vec['sb3'], in1=t["h"], op0=ALU.add, op1=ALU.add).then_inc(*mark("res_s", l))
                G = lambda l, i: gates[:, l, i, :].rearrange('p (c e) -> p c e', e=E)
                M = lambda l, i: gates[:, l, i, 0:8]
                wide = lambda ap, n=E: ap.rearrange('p (c o) -> p c o', o=1).to_broadcast([128, 8, n])
                pairs = lambda l, i: gates[:, l, i:i + 4, :].rearrange('p a b -> p (a b)').rearrange('p (c e f) -> p c e f', e=E, f=E)
                over_e = lambda l, i: gates[:, l, i, :].rearrange('p (c o f) -> p c o f', o=1, f=E).to_broadcast([128, 8, E, E])
                over_f = lambda l, i: gates[:, l, i, :].rearrange('p (c e o) -> p c e o', e=E, o=1).to_broadcast([128, 8, E, E])
                for l in range(2):
                    t = tiles[l]
                    tt(G(l, 0), ps[:, 4 * l + 2, 0:32].rearrange('p (c e) -> p c e', e=E), gbs[:, :].rearrange('p (o e) -> p o e', o=1).to_broadcast([128, 8, E]), ALU.add).then_inc(*mark("lg", l))
                for l in range(2):
                    t = tiles[l]
                    dve.wait_ge(*step("lg", turn, l))
                    dve.tensor_reduce(M(l, 3), G(l, 0), AX.X, ALU.max).then_inc(*mark("gmax", l))
                for l in range(2):
                    t = tiles[l]
                    dve.wait_ge(*step("gmax", turn, l))
                    tt(G(l, 1), G(l, 0), wide(M(l, 3)), ALU.subtract).then_inc(*mark("gsub", l))
                for l in range(2):
                    t = tiles[l]
                    dve.wait_ge(*step("gexp", turn, l))
                    dve.tensor_reduce(M(l, 4), G(l, 2), AX.X, ALU.add).then_inc(*mark("gsum", l))
                for l in range(2):
                    t = tiles[l]
                    dve.wait_ge(*step("gsum", turn, l))
                    dve.reciprocal(M(l, 5), M(l, 4)).then_inc(*mark("grec", l))
                for l in range(2):
                    t = tiles[l]
                    dve.wait_ge(*step("grec", turn, l))
                    tt(G(l, 6), G(l, 2), wide(M(l, 5)), ALU.mult).then_inc(*mark("gate", l))
                for l in range(2):
                    t = tiles[l]
                    dve.wait_ge(*step("gate", turn, l))
                    tt(pairs(l, 8), over_e(l, 6), over_f(l, 6), ALU.is_gt).then_inc(*mark("gt", l))
                for l in range(2):
                    t = tiles[l]
                    tt(pairs(l, 12), over_e(l, 6), over_f(l, 6), ALU.is_ge).then_inc(*mark("ge", l))
                for l in range(2):
                    t = tiles[l]
                    dve.wait_ge(*step("ge", turn, l))
                    tt(pairs(l, 12), pairs(l, 12), pairs(l, 8), ALU.subtract).then_inc(*mark("gd", l))
                for l in range(2):
                    t = tiles[l]
                    dve.wait_ge(*step("gd", turn, l))
                    tt(pairs(l, 12), pairs(l, 12), cs['earlier'].rearrange('p (o e f) -> p o e f', o=1, e=E).to_broadcast([128, 8, E, E]), ALU.mult).then_inc(*mark("gm", l))
                for l in range(2):
                    t = tiles[l]
                    dve.wait_ge(*step("gm", turn, l))
                    tt(pairs(l, 12), pairs(l, 12), pairs(l, 8), ALU.add).then_inc(*mark("gc", l))
                for l in range(2):
                    t = tiles[l]
                    dve.wait_ge(*step("gc", turn, l))
                    dve.tensor_reduce(gates[:, l, 7, :], pairs(l, 12), AX.X, ALU.add).then_inc(*mark("rank", l))
                for l in range(2):
                    t = tiles[l]
                    dve.wait_ge(*step("rank", turn, l))
                    dve.tensor_scalar(gates[:, l, 7, :], gates[:, l, 7, :], 2.0, None, ALU.is_lt).then_inc(*mark("sel", l))
                for l in range(2):
                    t = tiles[l]
                    dve.tensor_reduce(M(l, 3), G(l, 6), AX.X, ALU.max).then_inc(*mark("tmax", l))
                for l in range(2):
                    t = tiles[l]
                    dve.wait_ge(*step("tmax", turn, l))
                    tt(G(l, 16), G(l, 6), wide(M(l, 3)), ALU.subtract).then_inc(*mark("tsub", l))
                for l in range(2):
                    t = tiles[l]
                    dve.wait_ge(*step("topexp", turn, l))
                    tt(G(l, 18), G(l, 17), G(l, 7), ALU.mult).then_inc(*mark("tsel", l))
                for l in range(2):
                    t = tiles[l]
                    dve.wait_ge(*step("tsel", turn, l))
                    dve.tensor_reduce(M(l, 4), G(l, 18), AX.X, ALU.add).then_inc(*mark("tsum", l))
                for l in range(2):
                    t = tiles[l]
                    dve.wait_ge(*step("tsum", turn, l))
                    dve.reciprocal(M(l, 5), M(l, 4)).then_inc(*mark("trec", l))
                for l in range(2):
                    t = tiles[l]
                    dve.wait_ge(*step("trec", turn, l))
                    tt(G(l, 20), G(l, 18), wide(M(l, 5)), ALU.mult).then_inc(*mark("tgate", l))
                for l in range(2):
                    t = tiles[l]
                    dve.wait_ge(*step("eo0", turn, l))
                    dve.wait_ge(*step("spread0", turn, l))
                    tt(t["weighted"], t["expert_out"], P(l, 2), ALU.mult).then_inc(*mark("w0", l))
                for l in range(2):
                    t = tiles[l]
                    dve.wait_ge(*step("w0", turn, l))
                    tt(t["sum"], t["sum"], t["weighted"], ALU.add).then_inc(*mark("y0", l))
                for l in range(2):
                    t = tiles[l]
                    dve.wait_ge(*step("eo1", turn, l))
                    dve.wait_ge(*step("spread1", turn, l))
                    dve.wait_ge(*step("y0", turn, l))
                    tt(t["weighted"], t["expert_out"], P(l, 2), ALU.mult).then_inc(*mark("w1", l))
                for l in range(2):
                    t = tiles[l]
                    dve.wait_ge(*step("w1", turn, l))
                    tt(t["sum"], t["sum"], t["weighted"], ALU.add).then_inc(*mark("y1", l))
                for l in range(2):
                    t = tiles[l]
                    dve.wait_ge(*step("eo2", turn, l))
                    dve.wait_ge(*step("spread2", turn, l))
                    dve.wait_ge(*step("y1", turn, l))
                    tt(t["weighted"], t["expert_out"], P(l, 2), ALU.mult).then_inc(*mark("w2", l))
                for l in range(2):
                    t = tiles[l]
                    dve.wait_ge(*step("w2", turn, l))
                    tt(t["sum"], t["sum"], t["weighted"], ALU.add).then_inc(*mark("y2", l))
                for l in range(2):
                    t = tiles[l]
                    dve.wait_ge(*step("eo3", turn, l))
                    dve.wait_ge(*step("spread3", turn, l))
                    dve.wait_ge(*step("y2", turn, l))
                    tt(t["weighted"], t["expert_out"], P(l, 2), ALU.mult).then_inc(*mark("w3", l))
                for l in range(2):
                    t = tiles[l]
                    dve.wait_ge(*step("w3", turn, l))
                    tt(t["sum"], t["sum"], t["weighted"], ALU.add).then_inc(*mark("y3", l))
    return nc


_SQUARE = ("W_r", "W_k", "W_v", "A_w", "B_w", "A_a", "B_a", "W_o", "A_g", "B_g")


def layout(inputs):
    def a(name):
        return np.ascontiguousarray(np.asarray(inputs[name]))

    def modes(first, last):
        w = np.concatenate([a(first), a(last)], axis=3).transpose(0, 3, 1, 4, 2)
        return np.ascontiguousarray(w).reshape(LAYERS, NX, C, M2 * C)

    B = inputs["x"].shape[0]
    d = {
        "x": np.ascontiguousarray(a("x").reshape(B, HW, 3).transpose(0, 2, 1)),
        "ones": np.ones(HW, np.float32),
        "wr": modes("L0_tok_w1r", "L0_tok_w2r"),
        "wi": modes("L0_tok_w1i", "L0_tok_w2i"),
        "pw_w": np.ascontiguousarray(a("L0_tok_pw_w").transpose(0, 2, 1)),
    }
    for k in ("fc0_w", "fc0_b", "fc1_w", "fc1_b", "fc2_w", "fc2_b"):
        d[k] = a("L0_tok_" + k)
    for k in ("pw_b", "gamma", "beta"):
        d[k] = np.ascontiguousarray(a("L0_tok_" + k).T)
    for k in _SQUARE:
        d[k] = a("L0_attn_" + k)
    for k in ("sW1", "sW2", "sW3", "gW", "gb"):
        d[k] = a("L0_ffn_" + k)
    for e in range(E):
        for k in ("eW1", "eW2", "eW3"):
            d[f"{k}_{e}"] = a("L0_ffn_" + k)[e]

    def twice(v):
        return np.concatenate([v, v])

    v = {f"mix{i}": twice(a("L0_attn_x_mix")[i]) for i in range(6)}
    for k in ("b_w", "b_a", "k_k", "k_a", "r_k", "gn_w", "gn_b"):
        v[k] = twice(a("L0_attn_" + k))
    v["sb1"], v["sb2"], v["sb3"] = twice(a("L0_ffn_sb1")), a("L0_ffn_sb2"), twice(a("L0_ffn_sb3"))
    for e in range(E):
        v[f"eb1_{e}"] = a("L0_ffn_eb1")[e]
        v[f"eb2_{e}"] = twice(a("L0_ffn_eb2")[e])
        v[f"eb3_{e}"] = twice(a("L0_ffn_eb3")[e])
    d["vecs"] = np.stack(list(v.values()), axis=1)
    return d, list(v)


def kernel(**inputs):
    import concourse.bacc as _bacc
    from concourse.bass_utils import run_bass_kernel_spmd as _run

    nc = _bacc.Bacc("TRN2", target_bir_lowering=False, num_devices=1)
    arrays, vec_names = layout(inputs)
    B = inputs["x"].shape[0]
    fixed = constants()
    arrays["consts"] = np.ascontiguousarray(np.concatenate(list(fixed.values()), axis=1), dtype=np.float32)
    ins = {k: nc.dram_tensor("in_" + k, v.shape, F32, kind="ExternalInput").ap() for k, v in arrays.items()}
    out = nc.dram_tensor("out_0", [B, HH, WW], F32, kind="ExternalOutput").ap()
    spectra = nc.dram_tensor("spectra", [NX // 4, 2 * C, B, 4 * M2], F32, kind="Internal").ap()
    products = nc.dram_tensor("products", [B, NX, 2 * M2 * C], F32, kind="Internal").ap()
    field = nc.dram_tensor("field", [B // 2, 2, C, HW], F32, kind="Internal").ap()
    consts = {"ap": ins["consts"], "layout": [(k, v.shape[1]) for k, v in fixed.items()], "vecs": vec_names}
    x_spectra = nc.dram_tensor("x_spectra", [NX // 4, 2, 4, B, 4 * M2], F32, kind="Internal").ap()
    build(nc, B, ins, consts, out, spectra, products, field, x_spectra)
    r = _run(nc, [{"in_" + k: v for k, v in arrays.items()}], core_ids=[0])
    return r.results[0]["out_0"]
```
